# Optimizing a Trainium2 kernel written in Bass

```python
import numpy as np
import jax
import jax.numpy as jnp

def _softmax(x, axis=-1):
    return jax.nn.softmax(x, axis=axis)

def _gelu(x):
    return jax.nn.gelu(x, approximate=True)

def _silu(x):
    return jax.nn.silu(x)

def _sigmoid(x):
    return jax.nn.sigmoid(x)

def _layernorm(x, axis=-1, eps=1e-05):
    m = jnp.mean(x, axis=axis, keepdims=True)
    v = jnp.var(x, axis=axis, keepdims=True)
    return (x - m) / jnp.sqrt(v + eps)

def _scatter_add(tgt, idx, src, axis=0):
    return tgt.at[idx].add(src)

def _segment_sum(src, seg, n):
    return jax.ops.segment_sum(src, seg, n)
kernel_name = 'mk_gnn_preln_d4_gnn_r8_2dc07e'

def setup_inputs(seed: int=0):
    np.random.seed(seed)
    _w = jnp.asarray

    def _rec_inputs():
        import jax
        import jax.numpy as jnp
        _gk = jax.random.key(seed)
        x = -0.0005121 + 1.001 * jax.random.normal(jax.random.fold_in(_gk, 1), (6250, 64), jnp.float32)
        _s = jax.random.randint(jax.random.fold_in(_gk, 2), (100000,), 0, 6250, jnp.int32)
        _d = jax.random.randint(jax.random.fold_in(_gk, 3), (100000,), 0, 6250, jnp.int32)
        _loop = jnp.arange(6250, dtype=jnp.int32)
        src = jnp.concatenate([_s, _d, _loop])
        dst = jnp.concatenate([_d, _s, _loop])
        _o = jnp.argsort(dst, stable=True)
        src = src[_o]
        dst = dst[_o]
        edge_attr_16 = 0.000254156 + 0.999948 * jax.random.normal(jax.random.fold_in(_gk, 12), (206250, 16), jnp.float32)
        edge_attr_64 = -8.16379e-05 + 0.999858 * jax.random.normal(jax.random.fold_in(_gk, 13), (206250, 64), jnp.float32)
        edge_weight1 = 0.000452788 + 0.999756 * jax.random.normal(jax.random.fold_in(_gk, 15), (206250, 1), jnp.float32)
        return (x, src, dst, edge_attr_16, edge_attr_64, edge_weight1)
    x, src, dst, edge_attr_16, edge_attr_64, edge_weight1 = _rec_inputs()

    def _L0_gnn_setup():
        import jax, jax.numpy as jnp
        import numpy as np
        N = 6250
        M = 200000
        F = 64
        key = jax.random.key(seed)
        k1, k2, k3, k4 = jax.random.split(key, 4)
        reference = jax.random.normal(k1, (N, F), dtype=jnp.float32)
        edges = jax.random.normal(k2, (M, F), dtype=jnp.float32)
        attention = jax.random.normal(k3, (M, 1), dtype=jnp.float32)
        edge_index = jax.random.randint(k4, (2, M), 0, N, dtype=jnp.int32)
        return {'reference': reference, 'edges': edges, 'attention': attention, 'edge_index': edge_index}
    _L0_gnn_all = _L0_gnn_setup()
    _L0_gnn_in = {k: v for k, v in _L0_gnn_all.items() if k in ()}
    del _L0_gnn_all

    def _L1_gnn_setup():
        import jax, jax.numpy as jnp
        import numpy as np
        N = 6250
        E = 100000
        D = 64
        key = jax.random.key(seed)
        k1, k2, k3, k4, k5, k6 = jax.random.split(key, 6)
        node_feats = jax.random.normal(k1, (N, D), dtype=jnp.float32)
        edge_feats = jax.random.normal(k2, (E, D), dtype=jnp.float32)
        src = jax.random.randint(k3, (E,), 0, N, dtype=jnp.int32)
        dst = jnp.sort(jax.random.randint(k4, (E,), 0, N, dtype=jnp.int32))
        lim = 1.0 / np.sqrt(D)
        W = jax.random.uniform(k5, (D, D), minval=-lim, maxval=lim, dtype=jnp.float32)
        b = jax.random.uniform(k6, (D,), minval=-lim, maxval=lim, dtype=jnp.float32)
        return {'node_feats': node_feats, 'edge_feats': edge_feats, 'src': src, 'dst': dst, 'W': W, 'b': b}
    _L1_gnn_all = _L1_gnn_setup()
    _L1_gnn_in = {k: v for k, v in _L1_gnn_all.items() if k in ('W', 'b')}
    del _L1_gnn_all

    def _L2_gnn_setup():
        import jax, jax.numpy as jnp
        import numpy as np
        N = 6250
        D = 64
        L = 3
        DEG = 16
        SLOPE = 0.2
        key = jax.random.key(seed)
        ks = jax.random.split(key, 8)
        x = jax.random.normal(ks[0], (N, D), dtype=jnp.float32)
        E = N * DEG
        dst = jax.random.randint(ks[1], (E,), 0, N)
        off = jax.random.randint(ks[2], (E,), 1, N)
        src = (dst + off) % N
        loops = jnp.arange(N)
        edge_index = jnp.stack([jnp.concatenate([src, loops]), jnp.concatenate([dst, loops])]).astype(jnp.int64)
        s = 1.0 / np.sqrt(D)
        Wl = (jax.random.normal(ks[3], (L, D, D)) * s).astype(jnp.float32)
        Wr = (jax.random.normal(ks[4], (L, D, D)) * s).astype(jnp.float32)
        att = (jax.random.normal(ks[5], (L, D)) * s).astype(jnp.float32)
        bl = jnp.zeros((L, D), jnp.float32)
        br = jnp.zeros((L, D), jnp.float32)
        bias = jnp.zeros((L, D), jnp.float32)
        return dict(x=x, edge_index=edge_index, Wl=Wl, bl=bl, Wr=Wr, br=br, att=att, bias=bias)
    _L2_gnn_all = _L2_gnn_setup()
    _L2_gnn_in = {k: v for k, v in _L2_gnn_all.items() if k in ('Wl', 'bl', 'Wr', 'br', 'att', 'bias')}
    del _L2_gnn_all

    def _L3_gnn_setup():
        import jax, jax.numpy as jnp
        import numpy as np
        N, E, C, CE = (6250, 100000, 64, 16)
        NEG_SLOPE = 0.2
        key = jax.random.key(seed)
        k1, k2, k3, k4, k5 = jax.random.split(key, 5)
        x = jax.random.normal(k1, (N, C), dtype=jnp.float32)
        edge_index = jax.random.randint(k2, (2, E), 0, N, dtype=jnp.int64)
        edge_attr = jax.random.normal(k3, (E, CE), dtype=jnp.float32)
        bw = float(np.sqrt(6.0 / C))
        W = jax.random.uniform(k4, (C, C), minval=-bw, maxval=bw, dtype=jnp.float32)
        ba = float(np.sqrt(6.0 / (2 * C + CE)))
        w_att = jax.random.uniform(k5, (1, 2 * C + CE), minval=-ba, maxval=ba, dtype=jnp.float32)
        bias = jnp.zeros((C,), dtype=jnp.float32)
        return {'x': x, 'edge_index': edge_index, 'edge_attr': edge_attr, 'W': W, 'w_att': w_att, 'bias': bias}
    _L3_gnn_all = _L3_gnn_setup()
    _L3_gnn_in = {k: v for k, v in _L3_gnn_all.items() if k in ('W', 'w_att', 'bias')}
    del _L3_gnn_all
    return {'x': x, 'src': src, 'dst': dst, 'edge_attr_16': edge_attr_16, 'edge_attr_64': edge_attr_64, 'edge_weight1': edge_weight1, 'L1_gnn_W': _L1_gnn_in['W'], 'L1_gnn_b': _L1_gnn_in['b'], 'L2_gnn_Wl': _L2_gnn_in['Wl'], 'L2_gnn_bl': _L2_gnn_in['bl'], 'L2_gnn_Wr': _L2_gnn_in['Wr'], 'L2_gnn_br': _L2_gnn_in['br'], 'L2_gnn_att': _L2_gnn_in['att'], 'L2_gnn_bias': _L2_gnn_in['bias'], 'L3_gnn_W': _L3_gnn_in['W'], 'L3_gnn_w_att': _L3_gnn_in['w_att'], 'L3_gnn_bias': _L3_gnn_in['bias']}

def reference(x, src, dst, edge_attr_16, edge_attr_64, edge_weight1, L1_gnn_W, L1_gnn_b, L2_gnn_Wl, L2_gnn_bl, L2_gnn_Wr, L2_gnn_br, L2_gnn_att, L2_gnn_bias, L3_gnn_W, L3_gnn_w_att, L3_gnn_bias):
    import jax
    import jax.numpy as jnp

    def _L0_gnn_ref(reference, edges, attention, edge_index):
        import jax, jax.numpy as jnp
        import numpy as np
        N = 6250
        M = 200000
        F = 64
        idx = edge_index[0]
        a_exp = jnp.exp(attention)
        denom = jax.ops.segment_sum(a_exp, idx, num_segments=N)
        alpha = a_exp / denom[idx]
        weighted = edges * alpha
        out = jax.ops.segment_sum(weighted, idx, num_segments=N)
        return out

    def _L1_gnn_ref(node_feats, edge_feats, src, dst, W, b):
        import jax, jax.numpy as jnp
        import numpy as np
        N = 6250
        E = 100000
        D = 64
        m = node_feats[src] + edge_feats
        seg_max = jax.ops.segment_max(m, dst, num_segments=N)
        seg_max = jnp.where(jnp.isfinite(seg_max), seg_max, 0.0)
        ex = jnp.exp(m - seg_max[dst])
        denom = jax.ops.segment_sum(ex, dst, num_segments=N)
        a = ex / jnp.maximum(denom[dst], 1e-38)
        agg = jax.ops.segment_sum(m * a, dst, num_segments=N)
        out = jax.nn.relu(agg @ W.T + b) + node_feats
        return out

    def _L2_gnn_ref(x, edge_index, Wl, bl, Wr, br, att, bias):
        import jax, jax.numpy as jnp
        import numpy as np
        N = 6250
        D = 64
        L = 3
        DEG = 16
        SLOPE = 0.2
        src, dst = (edge_index[0], edge_index[1])
        n = x.shape[0]
        for l in range(L):
            xl = x @ Wl[l] + bl[l]
            xr = x @ Wr[l] + br[l]
            e = jax.nn.leaky_relu(xl[src] + xr[dst], SLOPE)
            logits = e @ att[l]
            m = jax.ops.segment_max(logits, dst, num_segments=n)
            ex = jnp.exp(logits - m[dst])
            denom = jax.ops.segment_sum(ex, dst, num_segments=n)
            alpha = ex / denom[dst]
            x = jax.ops.segment_sum(xl[src] * alpha[:, None], dst, num_segments=n) + bias[l]
            x = jax.nn.gelu(x, approximate=False)
        return x

    def _L3_gnn_ref(x, edge_index, edge_attr, W, w_att, bias):
        import jax, jax.numpy as jnp
        import numpy as np
        N, E, C, CE = (6250, 100000, 64, 16)
        NEG_SLOPE = 0.2
        n = x.shape[0]
        c = x.shape[1]
        ce = edge_attr.shape[1]
        h = x @ W
        src, dst = (edge_index[0], edge_index[1])
        x_i = h[dst]
        x_j = h[src]
        wa = w_att[0]
        alpha = x_i @ wa[:c] + edge_attr @ wa[c:c + ce] + x_j @ wa[c + ce:]
        alpha = jnp.where(alpha > 0, alpha, NEG_SLOPE * alpha)
        m = jax.ops.segment_max(alpha, dst, num_segments=n)
        m = jnp.where(jnp.isfinite(m), m, 0.0)
        a = jnp.exp(alpha - m[dst])
        s = jax.ops.segment_sum(a, dst, num_segments=n)
        a = a / (s[dst] + 1e-16)
        out = jax.ops.segment_sum(a[:, None] * x_j, dst, num_segments=n) + bias
        return out
    edge_index = jnp.stack([src, dst])
    h = jnp.maximum(_layernorm(x, axis=-1), 0.0)
    x = x + _L0_gnn_ref(h, edge_attr_64, edge_weight1, edge_index)
    h = jnp.maximum(_layernorm(x, axis=-1), 0.0)
    x = x + _L1_gnn_ref(h, edge_attr_64, src, dst, L1_gnn_W, L1_gnn_b)
    h = jnp.maximum(_layernorm(x, axis=-1), 0.0)
    x = x + _L2_gnn_ref(h, edge_index, L2_gnn_Wl, L2_gnn_bl, L2_gnn_Wr, L2_gnn_br, L2_gnn_att, L2_gnn_bias)
    h = jnp.maximum(_layernorm(x, axis=-1), 0.0)
    x = x + _L3_gnn_ref(h, edge_index, edge_attr_16, L3_gnn_W, L3_gnn_w_att, L3_gnn_bias)
    return x

_drawn_inputs = setup_inputs


def setup_inputs(seed=0):
    import zlib

    import numpy as np

    out = dict(_drawn_inputs(seed))
    spreads = {'L2_gnn_bl': (0.0, 0.1),
     'L2_gnn_br': (0.0, 0.8),
     'L2_gnn_bias': (0.0, 0.1),
     'L3_gnn_bias': (0.0, 0.1)}
    factors = {'L2_gnn_Wr': 8.0, 'L2_gnn_att': 8.0}
    for name, (base, spread) in spreads.items():
        noise = np.random.default_rng([zlib.crc32(name.encode()), seed]).standard_normal(out[name].shape)
        drawn = base * np.exp(spread * noise) if base else spread * noise
        out[name] = jnp.asarray(drawn.astype(out[name].dtype))
    for name, factor in factors.items():
        out[name] = (out[name] * factor).astype(out[name].dtype)
    return out
```

```python
from contextlib import ExitStack

import concourse.bass as bass
from concourse import mybir

ALU = mybir.AluOpType
ACT = mybir.ActivationFunctionType
AX = mybir.AxisListType.X
F32 = mybir.dt.float32
BF16 = mybir.dt.bfloat16
I32 = mybir.dt.int32

P = 128
N = 6250
D = 64
DE = 16
E = 206250
LAYERS = 3
KN = -(-N // P)
NODES = P * KN
TILES = -(-E // P)
ROWS = P * TILES
T = 26
CHUNKS = TILES // T
PAIRS = CHUNKS // 2
X = T + 1
G = 2
GROUPS = T // G
TABLES = 4
SW = D + 2
EMPTY = ROWS + P
ACC_ROWS = NODES + P
BIG = 1.0e38
SLOPE = 0.2
EPS = 1e-5
assert TILES % (2 * T) == 0 and (2 * T) % TABLES == 0 and T % G == 0

CREDIT = 2
READY, PREV, FREE = 1 + CREDIT, CREDIT, CREDIT - 1


class Steps:

    def __init__(self, eng, sem):
        self.eng, self.sem, self.done, self.turn, self.per_turn, self.n = eng, sem, 0, None, 0, 0

    def __call__(self, ins):
        ins.then_inc(self.sem, 1)
        self.n += 1

    def wait(self):
        if self.turn is None:
            self.eng.wait_ge(self.sem, self.done + self.n)
        else:
            self.eng.wait_ge(self.sem, self.turn * self.per_turn + (self.done + self.n))

    def enter(self, turn, per_turn):
        self.done, self.n, self.turn, self.per_turn = self.done + self.n, 0, turn, per_turn

    def leave(self, turns):
        assert self.n == self.per_turn, (self.n, self.per_turn)
        self.done, self.n, self.turn = self.done + self.n * turns, 0, None


def hold(eng):
    eng.nop(nofuse=True)


def bc(ap, shape, axis):
    return ap.unsqueeze(axis).to_broadcast(shape)


def turned(ap):
    return ap.rearrange("p a b -> p b a")


def setup_phase(nc, io, S):
    with nc.cleanup_on_exit(), ExitStack() as ctx:
        sb = lambda n, s, d: ctx.enter_context(nc.sbuf_tensor(n, s, d))
        sem = lambda n: nc.alloc_semaphore(n)
        jrow = sb("jrow", [P, P], I32)
        pcol = sb("pcol", [P, 1], I32)
        node_no = sb("node_no", [P, KN], I32)
        jf = sb("jf", [P, P], F32)
        loaded, iotas, steps = sem("loaded"), sem("iotas"), sem("setup_steps")
        block = ctx.enter_context(nc.Block())
        n_loads = 14

        @block.sync
        def _(sp):
            loads = [
                (S.src_i[:], io["src"]),
                (S.dst_i[:], io["dst"][1:ROWS + 1].rearrange("(p t) -> p t", p=P)),
                (S.prev_i[:], io["dst"][0:ROWS].rearrange("(p t) -> p t", p=P)),
                (S.xres[:], io["x"].rearrange("p (k f) -> p k f", f=D)),
                (S.ew[:], io["edge_w"]),
                (S.w1[:], io["w1t"]),
                (S.wlr[:], io["wlr"].rearrange("l k m -> k l m")),
                (S.w3[:], io["w3"]),
                (S.b1[:], io["b1"].to_broadcast([P, D])),
                (S.blr[:], io["blr"].to_broadcast([P, LAYERS * 2 * D])),
                (S.att[:], io["att"].to_broadcast([P, LAYERS * D])),
                (S.bias2[:], io["bias2"].to_broadcast([P, LAYERS * D])),
                (S.wa[:], io["wa"].to_broadcast([P, 2 * D + DE])),
                (S.bias3[:], io["bias3"].to_broadcast([P, D])),
            ]
            assert len(loads) == n_loads
            for dst, src in loads:
                sp.dma_start(dst, src).then_inc(loaded, 16)
            sp.wait_ge(loaded, 16 * n_loads)

        @block.gpsimd
        def _(pool):
            pool.iota(jrow[:], [[1, P]], 0, 0).then_inc(iotas, 1)
            pool.iota(pcol[:], [[0, 1]], 0, 1).then_inc(iotas, 1)
            pool.iota(node_no[:], [[1, KN]], ROWS, KN).then_inc(iotas, 1)

        @block.vector
        def _(v):
            st = Steps(v, steps)
            v.wait_ge(iotas, 3)
            st(v.tensor_copy(jf[:], jrow[:]))
            st(v.tensor_copy(S.pf[:], pcol[:]))
            st(v.tensor_copy(S.node_skip[:], node_no[:]))
            st(v.memset(S.ones[:], 1.0))
            st(v.memset(S.zeros[:], 0.0))
            st.wait()
            st(v.tensor_copy(S.col16[:], jf[:]))
            st(v.tensor_scalar(S.ident[:], jf[:], S.pf[:], None, ALU.is_equal))
            st(v.tensor_scalar(S.lower[:], jf[:], S.pf[:], None, ALU.is_lt))
            st(v.tensor_scalar(S.upto[:], jf[:], S.pf[:], None, ALU.is_ge))
            st(v.tensor_scalar(S.node_dump[:], S.pf[:], float(NODES), None, ALU.add))
            st(v.tensor_scalar(S.edge_dump[:], S.pf[:], float(ROWS), None, ALU.add))
            st(v.tensor_scalar(S.part_end[:], S.pf[:], float(TILES), float(TILES), ALU.mult, ALU.add))
            v.wait_ge(loaded, 16 * n_loads)
            st(v.tensor_copy(S.dst0[:], S.dst_i[:, 0:1]))
            st.wait()


def aggregate_phase(nc, io, S, R):
    with nc.cleanup_on_exit(), ExitStack() as ctx:
        sb = lambda n, s, d: ctx.enter_context(nc.sbuf_tensor(n, s, d))
        ps = lambda n, s: ctx.enter_context(nc.psum_tensor(n, s, F32))
        sem = lambda n: nc.alloc_semaphore(n)
        ex = sb("exp_w", [P, TILES], F32)
        part_i = sb("part_i", [P, 2, T], I32)
        part16 = sb("part16", [P, 2, T], BF16)
        dst_f, prev_f = sb("dst_f", [P, TILES], F32), sb("prev_f", [P, TILES], F32)
        ef = [sb(f"ef{b}", [P, T, D], F32) for b in range(2)]
        msg = [sb(f"msg{b}", [P, T, SW], F32) for b in range(2)]
        total = [sb(f"total{b}", [P, T, SW], F32) for b in range(2)]
        srcs = [sb(f"srcs{b}", [P, T], F32) for b in range(2)]
        lo1h = [sb(f"lo1h{b}", [P, T, P], BF16) for b in range(2)]
        hi1h = [sb(f"hi1h{b}", [P, T, KN], BF16) for b in range(2)]
        eq = [sb(f"eq{b}", [P, G, P], F32) for b in range(2)]
        earlier = sb("earlier", [P, G, P], F32)
        rank = sb("rank", [P, T], F32)
        target = sb("target", [P, T], F32)
        rows_i = [sb(f"rows_i{b}", [P, T], I32) for b in range(2)]
        row_of = [ps(f"row_of{b}", [P, G, P]) for b in range(2)]
        summed = [ps(f"summed{b}", [P, G, SW]) for b in range(2)]
        hist = ps("hist", [P, KN])
        prefix, seg_ps, s_ps = ps("prefix", [P, 2, KN]), ps("seg_ps", [KN, 3, P]), ps("s_ps", [D, P])
        tot, incl, tmp, last = [sb(f"seg_{n}", [P, KN], F32) for n in ("tot", "incl", "tmp", "last")]
        seg, segn = sb("seg", [P, 3, KN], F32), sb("segn", [P, 3, KN], F32)
        segt, segn_i = sb("segt", [KN, 3, P], I32), sb("segn_i", [P, 3, KN], I32)
        eh_f, cond = sb("eh_f", [P, 1], F32), sb("cond", [P, 1], F32)
        ef_in = [sem(f"ef_in{b}") for b in range(2)]
        names = ["exp_done", "msg_done", "srcs_done", "onehot_done", "weight_done", "row_of_done",
                 "eq_done", "summed_done", "total_done", "rows_done", "scattered", "zeroed",
                 "agg_steps", "hist_done", "hist_kept", "any_done", "counted", "prefix_done", "seg_ready", "seg_turned", "segt_ready", "seg_out", "seg_back", "heads_in"]
        q = {n: sem(n) for n in names}
        acc_done = [sem(f"acc_done{k}") for k in range(TABLES)]
        dump_rows = (R.state, R.state_so)
        block = ctx.enter_context(nc.Block())

        @block.sync
        def _(sp):
            feats = io["ea64"].rearrange("(p t) f -> p (t f)", p=P)
            inj = R.inject[0:ROWS].rearrange("(p t) f -> p (t f)", p=P)
            sp.dma_start(R.inject1[0:ROWS].rearrange("(p t) f -> p (t f)", p=P),
                         S.zeros[:, 0:TILES]).then_inc(q["zeroed"], 16)
            for table in dump_rows:
                sp.dma_start(table[ROWS:ROWS + P], S.zeros[:, 0:table.shape[1]]).then_inc(q["zeroed"], 16)
            sp.dma_start(R.state[EMPTY:EMPTY + 1, 0:D], S.zeros[0:1, 0:D]).then_inc(q["zeroed"], 16)
            sp.dma_start(R.state[EMPTY:EMPTY + 1, D:SW], S.ones[0:1, 0:2]).then_inc(q["zeroed"], 16)
            sp.dma_start(R.state_so[EMPTY:EMPTY + 1, 0:D], S.ones[0:1, 0:D]).then_inc(q["zeroed"], 16)
            sp.dma_start(R.state_so[EMPTY:EMPTY + 1, D:2 * D], S.zeros[0:1, 0:D]).then_inc(q["zeroed"], 16)
            with sp.Fori(0, PAIRS) as i:
                for b in range(2):
                    sp.wait_ge(q["msg_done"], i * 2 + (b + FREE))
                    sp.dma_start(ef[b][:].rearrange("p t f -> p (t f)"),
                                 feats[:, bass.ds(i * (2 * T * D) + b * T * D, T * D)]).then_inc(ef_in[b], 16)
                    sp.wait_ge(q["eq_done"], i * (2 * GROUPS) + (b * GROUPS + GROUPS // 2 + CREDIT))
                    sp.dma_start(inj[:, bass.ds(i * (2 * T * D) + b * T * D, T * D)],
                                 S.zeros[:, 0:T * D]).then_inc(q["zeroed"], 16)
            sp.wait_ge(q["segt_ready"], 1)
            sp.dma_start(R.seg_info.rearrange("s (q r) -> q s r", r=P), segt[:]).then_inc(q["seg_out"], 16)
            sp.dma_start(R.last_edge.rearrange("(q r) one -> q (r one)", r=P), segt[:, 0, :]).then_inc(q["seg_out"], 16)
            sp.wait_ge(q["seg_out"], 32)
            sp.dma_start(segn_i[:], R.seg_info.rearrange("s (p k) -> p s k", k=KN)).then_inc(q["seg_back"], 16)
            sp.wait_ge(q["zeroed"], 16 * (CHUNKS + 5 + len(dump_rows)))

        @block.gpsimd
        def _(pool):
            for k in range(TABLES):
                pool.dma_start(R.acc[k].rearrange("(p r) w -> p (r w)", p=P),
                               S.zeros[:, 0:ACC_ROWS // P * SW]).then_inc(acc_done[k], 16)
            pool.sem_inc(q["scattered"], 1)
            with pool.Fori(0, PAIRS) as i:
                for b in range(2):
                    pool.wait_ge(q["rows_done"], i * 2 + (b + READY))
                    hold(pool)
                    pool.wait_ge(q["total_done"], i * (2 * GROUPS) + ((b + 1) * GROUPS + CREDIT))
                    hold(pool)
                    for t in range(T):
                        g = b * T + t
                        k = g % TABLES
                        pool.wait_ge(acc_done[k], i * (2 * T // TABLES * 16) + (g // TABLES + 1) * 16)
                        hold(pool)
                        if t == TABLES:
                            pool.sem_inc(q["scattered"], 1)
                        pool.indirect_dma_start(
                            R.acc[k], bass.IndirectOffsetOnAxis(ap=rows_i[b][:, t:t + 1], axis=0),
                            total[b][:, t, :], None, compute_op=ALU.add).then_inc(acc_done[k], 16)
            pool.wait_ge(q["seg_out"], 32)
            pool.indirect_dma_start(S.head_i[:], None, R.last_edge,
                                    bass.IndirectOffsetOnAxis(ap=S.dst0[:], axis=0)).then_inc(q["heads_in"], 16)
            for k in range(TABLES):
                pool.wait_ge(acc_done[k], 16 * (1 + TILES // TABLES))

        @block.scalar
        def _(act):
            act.activation(ex[:], S.ew[:], ACT.Exp).then_inc(q["exp_done"], 1)
            act.wait_ge(q["exp_done"], 1)
            act.sem_inc(q["weight_done"], CREDIT)
            act.sem_inc(q["total_done"], CREDIT)
            with act.Fori(0, PAIRS) as i:
                for b in range(2):
                    act.wait_ge(q["summed_done"], i * (2 * GROUPS) + (b * GROUPS + 1))
                    hold(act)
                    act.activation(msg[b][:, :, D:D + 1],
                                   bc(ex[:, bass.ds(i * (2 * T) + b * T, T)], [P, T, 1], 2),
                                   ACT.Copy).then_inc(q["weight_done"], 1)
                    for g in range(GROUPS):
                        at = b * GROUPS + g
                        act.wait_ge(q["summed_done"], i * (2 * GROUPS) + (at + GROUPS + 2))
                        if g == 0:
                            hold(act)
                            act.wait_ge(q["scattered"], i * 2 + (b + 1))
                        act.activation(total[b][:, G * g:G * g + G, :], summed[at % 2][:],
                                       ACT.Copy).then_inc(q["total_done"], 1)
            act.wait_ge(q["hist_done"], 1)
            act.activation(S.count[:], hist[:], ACT.Copy).then_inc(q["hist_kept"], 1)
            act.wait_ge(q["hist_kept"], 1)

        @block.tensor
        def _(pe):
            pe.sem_inc(q["summed_done"], GROUPS + 1)
            pe.sem_inc(q["row_of_done"], CREDIT)
            pe.sem_inc(q["counted"], CREDIT)
            pe.matmul(hist[:], S.zeros[:, 0:P], S.zeros[:, 0:KN], start=True, stop=False,
                      skip_group_check=True)
            with pe.Fori(0, PAIRS) as i:
                for b in range(2):
                    pe.wait_ge(q["srcs_done"], i * 2 + (b + READY))
                    hold(pe)

                    def row_of_group(g):
                        at = b * GROUPS + g
                        pe.wait_ge(q["eq_done"], i * (2 * GROUPS) + (at + FREE))
                        for j in range(G):
                            t = G * g + j
                            last = pe.transpose(row_of[at % 2][:, j, :],
                                                srcs[b][:, t:t + 1].to_broadcast([P, P]), S.ident[:])
                        last.then_inc(q["row_of_done"], 1)

                    row_of_group(0)
                    for g in range(GROUPS):
                        at = b * GROUPS + g
                        if g + 1 < GROUPS:
                            row_of_group(g + 1)
                        if g == 0:
                            pe.wait_ge(q["msg_done"], i * 2 + (b + READY))
                            hold(pe)
                            pe.wait_ge(q["weight_done"], i * 2 + (b + READY))
                            hold(pe)
                        pe.wait_ge(q["total_done"], i * (2 * GROUPS) + (at + FREE))
                        hold(pe)
                        pe.wait_ge(q["eq_done"], i * (2 * GROUPS) + (at + READY))
                        for j in range(G):
                            t = G * g + j
                            last = pe.matmul(summed[at % 2][:, j, :], eq[at % 2][:, j, :],
                                             msg[b][:, t, :], start=True, stop=True,
                                             skip_group_check=True)
                        last.then_inc(q["summed_done"], 1)
                    pe.wait_ge(q["onehot_done"], i * 2 + (b + READY))
                    hold(pe)
                    for t in range(T):
                        last = pe.matmul(hist[:], lo1h[b][:, t, :], hi1h[b][:, t, :], start=False,
                                         stop=False, skip_group_check=True)
                    last.then_inc(q["counted"], 1)
            pe.matmul(hist[:], S.zeros[:, 0:P], S.zeros[:, 0:KN], start=False, stop=True,
                      skip_group_check=True).then_inc(q["hist_done"], 1)
            pe.wait_ge(q["hist_kept"], 1)
            pe.matmul(prefix[:, 0, :], S.upto[:], S.count[:], start=True, stop=True, skip_group_check=True)
            pe.matmul(prefix[:, 1, :], S.ones[:], S.count[:], start=True, stop=True,
                      skip_group_check=True).then_inc(q["prefix_done"], 1)
            pe.wait_ge(q["any_done"], 1)
            pe.transpose(s_ps[:], S.any_start[:].to_broadcast([P, D]), S.ident[:]).then_inc(q["prefix_done"], 1)
            pe.wait_ge(q["seg_ready"], 1)
            for s in range(3):
                last = pe.transpose(seg_ps[:, s, :], seg[:, s, :], S.ident[:])
            last.then_inc(q["seg_turned"], 1)

        def segments(v, st):
            v.wait_ge(q["prefix_done"], 2)
            st(v.tensor_scalar(S.pen_part[:], s_ps[:], -BIG, None, ALU.mult))
            st(v.tensor_copy(tot[:], prefix[:, 1, :]))
            st.wait()
            st(v.tensor_tensor_scan(incl[:], S.ones[:, 0:KN], tot[:], 0.0, ALU.mult, ALU.add))
            st.wait()
            st(v.tensor_tensor(incl[:], incl[:], tot[:], ALU.subtract))
            st.wait()
            st(v.tensor_tensor(tot[:], prefix[:, 0, :], incl[:], ALU.add))
            st.wait()
            st(v.tensor_scalar(seg[:, 0, :], tot[:], -1.0, 0.0, ALU.add, ALU.max))
            st(v.tensor_tensor(seg[:, 1, :], tot[:], S.count[:], ALU.subtract))
            st(v.tensor_copy(seg[:, 2, :], S.count[:]))
            st.wait()
            v.sem_inc(q["seg_ready"], 1)
            v.wait_ge(q["seg_turned"], 1)
            v.tensor_copy(segt[:], seg_ps[:]).then_inc(q["segt_ready"], 1)
            v.wait_ge(q["seg_back"], 16)
            st(v.tensor_copy(segn[:], segn_i[:]))
            st.wait()
            st(v.tensor_scalar(segn[:, 2, :], segn[:, 2, :], 0.0, None, ALU.is_equal))
            st(v.tensor_tensor(tmp[:], S.node_skip[:], segn[:, 1, :], ALU.subtract))
            st(v.tensor_scalar(last[:], segn[:, 0, :], -1.0, float(EMPTY), ALU.mult, ALU.add))
            st.wait()
            st(v.tensor_tensor(last[:], last[:], segn[:, 2, :], ALU.mult))
            st.wait()
            st(v.tensor_tensor(last[:], last[:], segn[:, 0, :], ALU.add))
            st.wait()
            st(v.tensor_copy(S.end_i[:], last[:]))
            st(v.tensor_tensor(tmp[:], tmp[:], segn[:, 2, :], ALU.mult))
            st.wait()
            st(v.tensor_tensor(tmp[:], tmp[:], segn[:, 1, :], ALU.add))
            st.wait()
            st(v.tensor_copy(S.start_i[:], tmp[:]))
            v.wait_ge(q["heads_in"], 16)
            st(v.tensor_copy(eh_f[:], S.head_i[:]))
            st.wait()
            st(v.tensor_tensor(cond[:], eh_f[:], S.part_end[:], ALU.is_lt))
            st.wait()
            st(v.tensor_tensor(cond[:], cond[:], S.keep[:, 1:2], ALU.mult))
            st(v.tensor_tensor(eh_f[:], eh_f[:], S.edge_dump[:], ALU.subtract))
            st.wait()
            st(v.tensor_tensor(eh_f[:], eh_f[:], cond[:], ALU.mult))
            st.wait()
            st(v.tensor_tensor(eh_f[:], eh_f[:], S.edge_dump[:], ALU.add))
            st.wait()
            st(v.tensor_copy(S.mend_i[:], eh_f[:]))
            st.wait()

        @block.vector
        def _(v):
            st = Steps(v, q["agg_steps"])
            v.sem_inc(q["msg_done"], CREDIT)
            v.sem_inc(q["srcs_done"], CREDIT)
            v.sem_inc(q["onehot_done"], CREDIT)
            v.sem_inc(q["eq_done"], CREDIT)
            v.sem_inc(q["rows_done"], CREDIT)
            for b in range(2):
                st(v.memset(msg[b][:, :, D + 1:SW], 0.0))
            v.wait_ge(q["exp_done"], 1)
            per_turn = 2 * (2 * GROUPS + 3 + 1 + 3)
            with v.Fori(0, PAIRS) as i:
                st.enter(i, per_turn)
                for b in range(2):
                    c0 = i * (2 * T) + b * T
                    v.wait_ge(q["summed_done"], i * (2 * GROUPS) + (b * GROUPS + 1))
                    v.tensor_scalar(srcs[b][:], S.src_i[:, bass.ds(c0, T)], 0.0, None,
                                    ALU.add).then_inc(q["srcs_done"], 1)
                    v.wait_ge(ef_in[b], i * 16 + 16)
                    v.tensor_tensor(msg[b][:, :, 0:D], ef[b][:], bc(ex[:, bass.ds(c0, T)], [P, T, D], 2),
                                    ALU.mult).then_inc(q["msg_done"], 1)
                    v.wait_ge(q["srcs_done"], i * 2 + (b + READY))
                    for g in range(GROUPS):
                        at = b * GROUPS + g
                        v.wait_ge(q["row_of_done"], i * (2 * GROUPS) + (at + READY))
                        v.wait_ge(q["summed_done"], i * (2 * GROUPS) + (at + GROUPS))
                        v.tensor_tensor(eq[at % 2][:], row_of[at % 2][:],
                                        bc(srcs[b][:, G * g:G * g + G], [P, G, P], 2),
                                        ALU.is_equal).then_inc(q["eq_done"], 1)
                        v.wait_ge(q["eq_done"], i * (2 * GROUPS) + (at + READY))
                        st(v.tensor_tensor(earlier[:], eq[at % 2][:], bc(S.lower[:], [P, G, P], 1), ALU.mult))
                        st.wait()
                        st(v.tensor_reduce(rank[:, G * g:G * g + G], earlier[:], AX, ALU.add))
                        st.wait()
                    st(v.tensor_scalar(rank[:], rank[:], 1.0, None, ALU.min))
                    st(v.tensor_scalar(target[:], srcs[b][:], -1.0, S.node_dump[:], ALU.mult, ALU.add))
                    st.wait()
                    st(v.tensor_tensor(target[:], target[:], rank[:], ALU.mult))
                    st.wait()
                    st(v.tensor_tensor(target[:], target[:], srcs[b][:], ALU.add))
                    st.wait()
                    v.wait_ge(q["scattered"], i * 2 + (b + 1))
                    v.tensor_copy(rows_i[b][:], target[:]).then_inc(q["rows_done"], 1)
                    st(v.tensor_scalar(part_i[:, 0, :], S.dst_i[:, bass.ds(c0, T)], P - 1, None, ALU.bitwise_and))
                    st(v.tensor_scalar(part_i[:, 1, :], S.dst_i[:, bass.ds(c0, T)], P.bit_length() - 1, None,
                                       ALU.arith_shift_right))
                    st.wait()
                    st(v.tensor_copy(part16[:], part_i[:]))
                    st.wait()
                    v.wait_ge(q["counted"], i * 2 + (b + FREE))
                    v.tensor_tensor(hi1h[b][:], bc(S.col16[:, 0:KN], [P, T, KN], 1),
                                    bc(part16[:, 1, :], [P, T, KN], 2), ALU.is_equal)
                    v.tensor_tensor(lo1h[b][:], bc(S.col16[:], [P, T, P], 1),
                                    bc(part16[:, 0, :], [P, T, P], 2),
                                    ALU.is_equal).then_inc(q["onehot_done"], 1)
                    v.wait_ge(q["rows_done"], i * 2 + (b + READY))
                st.leave(PAIRS)
            st(v.tensor_copy(dst_f[:], S.dst_i[:]))
            st(v.tensor_copy(prev_f[:], S.prev_i[:]))
            st.wait()
            st(v.tensor_tensor(dst_f[:], dst_f[:], prev_f[:], ALU.not_equal))
            st.wait()
            begin = dst_f[:].rearrange("p (c t) -> p c t", t=T)
            pen = S.pen[:].rearrange("p (c x) -> p c x", x=X)
            keep = S.keep[:].rearrange("p (c x) -> p c x", x=X)
            v.tensor_reduce(S.any_start[:], dst_f[:], AX, ALU.max).then_inc(q["any_done"], 1)
            st(v.tensor_scalar(pen[:, :, 1:X], begin, -BIG, None, ALU.mult))
            st(v.memset(pen[:, :, 0:1], -BIG))
            st(v.tensor_scalar(keep[:, :, 1:X], begin, -1.0, 1.0, ALU.mult, ALU.add))
            st(v.memset(keep[:, :, 0:1], 0.0))
            st.wait()
            segments(v, st)


GK = 4
NODE_GROUPS = [(k, min(GK, KN - k)) for k in range(0, KN, GK)]


def skewed(order):
    for now in range(len(NODE_GROUPS) + max(late for run, late in order)):
        for run, late in order:
            if 0 <= now - late < len(NODE_GROUPS):
                run(now - late)


class Linear:

    def __init__(self, ctx, nc, tag, width):
        self.turned = [ctx.enter_context(nc.psum_tensor(f"{tag}_turned{b}", [D, GK, P], F32)) for b in range(2)]
        self.out = [ctx.enter_context(nc.psum_tensor(f"{tag}_out{b}", [P, GK, width], F32)) for b in range(2)]
        self.col = [ctx.enter_context(nc.sbuf_tensor(f"{tag}_col{b}", [D, GK, P], F32)) for b in range(2)]
        sem = lambda n: nc.alloc_semaphore(f"{tag}_{n}")
        self.turned_done, self.col_done, self.out_done, self.taken = sem("turned"), sem("col"), sem("out"), sem("taken")

    def turn(self, pe, g, a, a_done, ident):
        k0, n = NODE_GROUPS[g]
        pe.wait_ge(a_done, g + 1)
        if g >= 2:
            pe.wait_ge(self.col_done, g - 1)
        for k in range(n):
            last = pe.transpose(self.turned[g % 2][:, k, :], a[:, k0 + k, :], ident)
        last.then_inc(self.turned_done, 1)

    def copy(self, act, g):
        k0, n = NODE_GROUPS[g]
        act.wait_ge(self.turned_done, g + 1)
        if g >= 2:
            act.wait_ge(self.out_done, g - 1)
        act.activation(self.col[g % 2][:, 0:n, :], self.turned[g % 2][:, 0:n, :],
                       ACT.Copy).then_inc(self.col_done, 1)

    def multiply(self, pe, g, weight, bias, ones):
        k0, n = NODE_GROUPS[g]
        pe.wait_ge(self.col_done, g + 1)
        if g >= 2:
            pe.wait_ge(self.taken, g - 1)
        for k in range(n):
            last = pe.matmul(self.out[g % 2][:, k, :], self.col[g % 2][:, k, :], weight,
                             start=True, stop=bias is None, skip_group_check=True)
            if bias is not None:
                last = pe.matmul(self.out[g % 2][:, k, :], ones, bias, start=False, stop=True,
                                 skip_group_check=True)
        last.then_inc(self.out_done, 1)

    def take(self, act, g, out, func):
        k0, n = NODE_GROUPS[g]
        act.wait_ge(self.out_done, g + 1)
        act.activation(out[:, k0:k0 + n, :], self.out[g % 2][:, 0:n, :], func).then_inc(self.taken, 1)


class Scratch:
    pass


def node_rows(table):
    return table.rearrange("(p k) f -> p k f", k=KN)


def index_chunk(io, c):
    return io["src"][:, bass.ds(c * T, T)]


def gather_loop(pool, idx, rows, table, idx_in, landed, used):
    with pool.Fori(0, PAIRS) as i:
        for b in range(2):
            pool.wait_ge(used, i * 2 + (b + FREE))
            hold(pool)
            pool.wait_ge(idx_in[b], i * 16 + 16)
            hold(pool)
            for t in range(T):
                pool.indirect_dma_start(rows[b][:, t, :], None, table,
                                        bass.IndirectOffsetOnAxis(ap=idx[b][:, t:t + 1], axis=0)
                                        ).then_inc(landed[b], 16)


def feature_softmax_phase(nc, io, S, R):
    with nc.cleanup_on_exit(), ExitStack() as ctx:
        sb = lambda n, s: ctx.enter_context(nc.sbuf_tensor(n, s, F32))
        sem = lambda n: nc.alloc_semaphore(n)
        idx = [ctx.enter_context(nc.sbuf_tensor(f"idx{b}", [P, T], I32)) for b in range(2)]
        rows = [sb(f"rows{b}", [P, T, D]) for b in range(2)]
        ef = [sb(f"ef1_{b}", [P, T, D]) for b in range(2)]
        m, pen, mx, dec, wgt, ssum, y, osum = [sb(f"f1_{n}", [P, D, X]) for n in
                                               ("m", "pen", "mx", "dec", "wgt", "ssum", "y", "osum")]
        out_so = [sb(f"out_so{b}", [P, T, 2 * D]) for b in range(2)]
        out_m = [sb(f"out_m{b}", [P, T, D]) for b in range(2)]
        landed = [sem(f"landed{b}") for b in range(2)]
        idx_in = [sem(f"idx_in{b}") for b in range(2)]
        ef_in = [sem(f"ef1_in{b}") for b in range(2)]
        names = ["m_done", "pen_done", "mx_done", "dec_ask", "dec_done", "wgt_ask", "wgt_done",
                 "ssum_done", "y_done", "osum_done", "out_m_done", "out_s_done", "out_o_done", "f1_steps",
                 "f1_init"]
        q = {n: sem(n) for n in names}
        kept = [sem(f"kept{b}") for b in range(2)]
        block = ctx.enter_context(nc.Block())
        flat = lambda t: t[:].rearrange("p f x -> p (f x)")

        @block.sync
        def _(sp):
            feats = io["ea64"].rearrange("(p t) f -> p (t f)", p=P)
            so = R.state_so[0:ROWS].rearrange("(p t) w -> p (t w)", p=P)
            sm = R.state_m[0:ROWS].rearrange("(p t) w -> p (t w)", p=P)
            for b in range(2):
                sp.dma_start(idx[b][:], index_chunk(io, b)).then_inc(idx_in[b], 16)
            for b in range(2):
                sp.dma_start(ef[b][:].rearrange("p t f -> p (t f)"), feats[:, b * T * D:(b + 1) * T * D]).then_inc(ef_in[b], 16)
                sp.sem_inc(kept[b], 16)
            with sp.Fori(0, PAIRS - 1) as i:
                for b in range(2):
                    sp.wait_ge(landed[b], i * (T * 16) + T * 16)
                    sp.dma_start(idx[b][:], index_chunk(io, i * 2 + (b + 2))).then_inc(idx_in[b], 16)
                    sp.wait_ge(q["m_done"], i * 2 + (b + READY))
                    sp.dma_start(ef[b][:].rearrange("p t f -> p (t f)"),
                                 feats[:, bass.ds(i * (2 * T * D) + (b + 2) * T * D, T * D)]).then_inc(ef_in[b], 16)
                    sp.wait_ge(q["out_o_done"], i * 2 + (b + READY))
                    sp.dma_start(so[:, bass.ds(i * (4 * T * D) + b * 2 * T * D, 2 * T * D)],
                                 out_so[b][:].rearrange("p t f -> p (t f)")).then_inc(kept[b], 16)
                    sp.dma_start(sm[:, bass.ds(i * (2 * T * D) + b * T * D, T * D)],
                                 out_m[b][:].rearrange("p t f -> p (t f)")).then_inc(kept[b], 16)
            for b in range(2):
                c = 2 * (PAIRS - 1) + b
                sp.wait_ge(q["out_o_done"], c + READY)
                sp.dma_start(so[:, c * 2 * T * D:(c + 1) * 2 * T * D],
                             out_so[b][:].rearrange("p t f -> p (t f)")).then_inc(kept[b], 16)
                sp.dma_start(sm[:, c * T * D:(c + 1) * T * D],
                             out_m[b][:].rearrange("p t f -> p (t f)")).then_inc(kept[b], 16)
            for b in range(2):
                sp.wait_ge(kept[b], 16 + 32 * PAIRS)

        @block.gpsimd
        def _(pool):
            gather_loop(pool, idx, rows, R.table, idx_in, landed, q["m_done"])

        @block.scalar
        def _(act):
            for n in ("pen_done", "dec_done", "wgt_done", "out_m_done", "out_s_done", "out_o_done"):
                act.sem_inc(q[n], CREDIT)
            act.wait_ge(q["f1_init"], 1)
            with act.Fori(0, PAIRS) as i:
                for b in range(2):
                    c = lambda k: i * 2 + (b + k)
                    act.wait_ge(q["dec_ask"], c(PREV))
                    hold(act)
                    act.activation(pen[:], bc(S.pen[:, bass.ds(i * (2 * X) + b * X, X)], [P, D, X], 1),
                                   ACT.Copy).then_inc(q["pen_done"], 1)
                    act.wait_ge(q["mx_done"], c(READY))
                    act.wait_ge(kept[b], i * 32 + 16)
                    act.activation(turned(out_m[b][:]), mx[:, :, 1:X], ACT.Copy).then_inc(q["out_m_done"], 1)
                    act.wait_ge(q["dec_ask"], c(READY))
                    act.activation(dec[:, :, 1:X], dec[:, :, 1:X], ACT.Exp).then_inc(q["dec_done"], 1)
                    act.wait_ge(q["wgt_ask"], c(READY))
                    act.activation(wgt[:, :, 1:X], wgt[:, :, 1:X], ACT.Exp).then_inc(q["wgt_done"], 1)
                    act.wait_ge(q["ssum_done"], c(READY))
                    act.activation(turned(out_so[b][:, :, 0:D]), ssum[:, :, 1:X], ACT.Copy).then_inc(q["out_s_done"], 1)
                    act.wait_ge(q["osum_done"], c(READY))
                    act.activation(turned(out_so[b][:, :, D:2 * D]), osum[:, :, 1:X], ACT.Copy).then_inc(q["out_o_done"], 1)
                    act.wait_ge(q["out_m_done"], c(READY))
                    act.wait_ge(q["out_s_done"], c(READY))
                    hold(act)

        @block.vector
        def _(v):
            st = Steps(v, q["f1_steps"])
            for n in ("m_done", "mx_done", "dec_ask", "wgt_ask", "ssum_done", "y_done", "osum_done"):
                v.sem_inc(q[n], CREDIT)
            st(v.memset(mx[:], -BIG))
            st(v.memset(ssum[:], 0.0))
            st(v.memset(osum[:], 0.0))
            st(v.memset(dec[:], 0.0))
            st.wait()
            v.sem_inc(q["f1_init"], 1)
            with v.Fori(0, PAIRS) as i:
                st.enter(i, 2 * 4)
                for b in range(2):
                    c = lambda k: i * 2 + (b + k)
                    v.wait_ge(landed[b], i * (T * 16) + T * 16)
                    hold(v)
                    v.wait_ge(ef_in[b], i * 16 + 16)
                    v.tensor_tensor(turned(m[:, :, 1:X]), rows[b][:], ef[b][:], ALU.add).then_inc(q["m_done"], 1)
                    st(v.tensor_copy(m[:, :, 0:1], mx[:, :, T:X]))
                    v.wait_ge(q["m_done"], c(READY))
                    hold(v)
                    v.wait_ge(q["out_m_done"], c(PREV))
                    hold(v)
                    v.wait_ge(q["pen_done"], c(READY))
                    hold(v)
                    st.wait()
                    v.tensor_tensor_scan(flat(mx), flat(pen), flat(m), 0.0, ALU.add, ALU.max).then_inc(q["mx_done"], 1)
                    v.wait_ge(q["mx_done"], c(READY))
                    hold(v)
                    v.wait_ge(q["osum_done"], c(PREV))
                    st(v.tensor_tensor(dec[:, :, 1:X], mx[:, :, 0:T], pen[:, :, 1:X], ALU.add))
                    st.wait()
                    v.tensor_tensor(dec[:, :, 1:X], dec[:, :, 1:X], mx[:, :, 1:X], ALU.subtract).then_inc(q["dec_ask"], 1)
                    v.tensor_tensor(wgt[:, :, 1:X], m[:, :, 1:X], mx[:, :, 1:X], ALU.subtract).then_inc(q["wgt_ask"], 1)
                    st(v.tensor_copy(wgt[:, :, 0:1], ssum[:, :, T:X]))
                    v.wait_ge(q["dec_done"], c(READY))
                    hold(v)
                    v.wait_ge(q["out_s_done"], c(PREV))
                    hold(v)
                    v.wait_ge(q["wgt_done"], c(READY))
                    hold(v)
                    st.wait()
                    v.tensor_tensor_scan(flat(ssum), flat(dec), flat(wgt), 0.0, ALU.mult, ALU.add).then_inc(q["ssum_done"], 1)
                    v.tensor_tensor(y[:, :, 1:X], m[:, :, 1:X], wgt[:, :, 1:X], ALU.mult).then_inc(q["y_done"], 1)
                    st(v.tensor_copy(y[:, :, 0:1], osum[:, :, T:X]))
                    v.wait_ge(q["y_done"], c(READY))
                    hold(v)
                    v.wait_ge(q["out_o_done"], c(PREV))
                    hold(v)
                    st.wait()
                    v.tensor_tensor_scan(flat(osum), flat(dec), flat(y), 0.0, ALU.mult, ALU.add).then_inc(q["osum_done"], 1)
                    v.wait_ge(q["osum_done"], c(READY))
                    hold(v)
                    v.wait_ge(q["ssum_done"], c(READY))
                    hold(v)
                st.leave(PAIRS)
            for n, tile in enumerate((mx, ssum, osum)):
                st(v.tensor_copy(S.final[:, n, :], tile[:, :, T]))
            st.wait()


def scalar_softmax_phase(nc, io, S, R, layer):
    gat = layer == LAYERS
    tag = f"e{layer}"
    GW = SW if gat else D
    with nc.cleanup_on_exit(), ExitStack() as ctx:
        sb = lambda n, s: ctx.enter_context(nc.sbuf_tensor(f"{tag}_{n}", s, F32))
        sem = lambda n: nc.alloc_semaphore(f"{tag}_{n}")
        idx = [ctx.enter_context(nc.sbuf_tensor(f"{tag}_idx{b}", [P, T], I32)) for b in range(2)]
        rows = [sb(f"rows{b}", [P, T, GW]) for b in range(2)]
        FW = DE if gat else D
        side = [sb(f"side{b}", [P, T, FW]) for b in range(2)]
        if gat:
            inj1, keep1, dst_score = sb("inj1", [P, TILES]), sb("keep1", [P, TILES]), sb("dst_score", [P, TILES])
            z = sb("z", [P, T, DE])
        else:
            kx, inj, xr = sb("kx", [P, D, X]), sb("inj", [P, D, X]), sb("xr", [P, D, X])
            z = sb("z", [P, T, D])
        score, mrow, srow, e2 = sb("score", [P, X]), sb("mrow", [P, X]), sb("srow", [P, X]), sb("e2", [P, 2, X])
        dx, y, osum = sb("dx", [P, D, X]), sb("y", [P, D, X]), sb("osum", [P, D, X])
        out = [sb(f"out{b}", [P, T, SW]) for b in range(2)]
        landed = [sem(f"landed{b}") for b in range(2)]
        idx_in = [sem(f"idx_in{b}") for b in range(2)]
        side_in = [sem(f"side_in{b}") for b in range(2)]
        kept = [sem(f"kept{b}") for b in range(2)]
        names = ["kx_done", "inj_done", "xr_done", "z_done", "exp_ask", "exp_done", "dx_done", "y_done",
                 "srow_done", "osum_done", "out_sm_done", "out_o_done", "steps", "init", "inj1_in", "fdot_done"]
        q = {n: sem(n) for n in names}
        block = ctx.enter_context(nc.Block())
        flat = lambda t: t[:].rearrange("p f x -> p (f x)")
        side_used = q["fdot_done"] if gat else q["inj_done"]

        @block.sync
        def _(sp):
            src = io["ea16"] if gat else R.inject[0:ROWS]
            feats = src.rearrange("(p t) f -> p (t f)", p=P)
            states = R.state[0:ROWS].rearrange("(p t) w -> p (t w)", p=P)
            W = T * FW
            if gat:
                sp.dma_start(inj1[:], R.inject1[0:ROWS].rearrange("(p t) f -> p (t f)", p=P)).then_inc(q["inj1_in"], 16)
            for b in range(2):
                sp.dma_start(idx[b][:], index_chunk(io, b)).then_inc(idx_in[b], 16)
            for b in range(2):
                sp.dma_start(side[b][:].rearrange("p t f -> p (t f)"), feats[:, b * W:(b + 1) * W]).then_inc(side_in[b], 16)
                sp.sem_inc(kept[b], 16)
            with sp.Fori(0, PAIRS - 1) as i:
                for b in range(2):
                    sp.wait_ge(landed[b], i * (T * 16) + T * 16)
                    sp.dma_start(idx[b][:], index_chunk(io, i * 2 + (b + 2))).then_inc(idx_in[b], 16)
                    sp.wait_ge(side_used, i * 2 + (b + READY))
                    sp.dma_start(side[b][:].rearrange("p t f -> p (t f)"),
                                 feats[:, bass.ds(i * (2 * W) + (b + 2) * W, W)]).then_inc(side_in[b], 16)
                    sp.wait_ge(q["out_sm_done"], i * 2 + (b + READY))
                    hold(sp)
                    sp.wait_ge(q["out_o_done"], i * 2 + (b + READY))
                    sp.dma_start(states[:, bass.ds(i * (2 * T * SW) + b * T * SW, T * SW)],
                                 out[b][:].rearrange("p t f -> p (t f)")).then_inc(kept[b], 16)
            for b in range(2):
                c = 2 * (PAIRS - 1) + b
                sp.wait_ge(q["out_sm_done"], c + READY)
                sp.wait_ge(q["out_o_done"], c + READY)
                sp.dma_start(states[:, c * T * SW:(c + 1) * T * SW],
                             out[b][:].rearrange("p t f -> p (t f)")).then_inc(kept[b], 16)
            for b in range(2):
                sp.wait_ge(kept[b], 16 + 16 * PAIRS)

        @block.gpsimd
        def _(pool):
            table = R.table3 if gat else R.table
            gather_loop(pool, idx, rows, table, idx_in, landed, q["y_done"])

        @block.scalar
        def _(act):
            for n in ("kx_done", "inj_done", "exp_done", "dx_done", "out_o_done"):
                act.sem_inc(q[n], CREDIT)
            act.wait_ge(q["init"], 1)
            with act.Fori(0, PAIRS) as i:
                for b in range(2):
                    c = lambda k: i * 2 + (b + k)
                    if not gat:
                        act.wait_ge(q["xr_done"], c(PREV))
                        hold(act)
                        act.activation(kx[:], bc(S.keep[:, bass.ds(i * (2 * X) + b * X, X)], [P, D, X], 1),
                                       ACT.Copy).then_inc(q["kx_done"], 1)
                        act.wait_ge(side_in[b], i * 16 + 16)
                        act.activation(inj[:, :, 1:X], turned(side[b][:]), ACT.Copy).then_inc(q["inj_done"], 1)
                    act.wait_ge(q["exp_ask"], c(READY))
                    act.activation(e2[:, :, 1:X], e2[:, :, 1:X], ACT.Exp).then_inc(q["exp_done"], 1)
                    act.wait_ge(q["osum_done"], c(PREV))
                    hold(act)
                    act.wait_ge(q["exp_done"], c(READY))
                    act.activation(dx[:], bc(e2[:, 0, :], [P, D, X], 1), ACT.Copy).then_inc(q["dx_done"], 1)
                    act.wait_ge(kept[b], i * 16 + 16)
                    hold(act)
                    act.wait_ge(q["osum_done"], c(READY))
                    act.activation(turned(out[b][:, :, 0:D]), osum[:, :, 1:X], ACT.Copy).then_inc(q["out_o_done"], 1)

        @block.vector
        def _(v):
            st = Steps(v, q["steps"])
            for n in ("xr_done", "z_done", "exp_ask", "y_done", "srow_done", "osum_done", "out_sm_done", "fdot_done"):
                v.sem_inc(q[n], CREDIT)
            st(v.memset(mrow[:], -BIG))
            st(v.memset(srow[:], 0.0))
            st(v.memset(osum[:], 0.0))
            st(v.memset(e2[:], 0.0))
            if gat:
                st(v.tensor_copy(keep1[:].rearrange("p (c t) -> p c t", t=T),
                                 S.keep[:].rearrange("p (c x) -> p c x", x=X)[:, :, 1:X]))
                v.wait_ge(q["inj1_in"], 16)
                st.wait()
                st(v.tensor_tensor_scan(dst_score[:], keep1[:], inj1[:], S.head_row[:, D + 1:D + 2], ALU.mult, ALU.add))
            else:
                st(v.tensor_copy(xr[:, :, T], S.head_row[:, 0:D]))
            st.wait()
            v.sem_inc(q["init"], 1)
            per_chunk = 11
            with v.Fori(0, PAIRS) as i:
                st.enter(i, 2 * per_chunk)
                for b in range(2):
                    c = lambda k: i * 2 + (b + k)
                    pen = S.pen[:, bass.ds(i * (2 * X) + b * X, X)]
                    if gat:
                        v.wait_ge(side_in[b], i * 16 + 16)
                        v.tensor_tensor(z[:], side[b][:], bc(S.wa[:, D:D + DE], [P, T, DE], 1),
                                        ALU.mult).then_inc(q["fdot_done"], 1)
                        v.wait_ge(q["fdot_done"], c(READY))
                        hold(v)
                        st(v.tensor_reduce(score[:, 1:X], z[:], AX, ALU.add))
                        v.wait_ge(landed[b], i * (T * 16) + T * 16)
                        hold(v)
                        st.wait()
                        st(v.tensor_tensor(score[:, 1:X], score[:, 1:X], rows[b][:, :, D], ALU.add))
                        st.wait()
                        st(v.tensor_tensor(score[:, 1:X], score[:, 1:X], dst_score[:, bass.ds(i * (2 * T) + b * T, T)], ALU.add))
                        st.wait()
                        st(v.scalar_tensor_tensor(score[:, 1:X], score[:, 1:X], SLOPE, score[:, 1:X], ALU.mult, ALU.max))
                    else:
                        v.wait_ge(q["kx_done"], c(READY))
                        hold(v)
                        v.wait_ge(q["inj_done"], c(READY))
                        hold(v)
                        st(v.tensor_copy(inj[:, :, 0], xr[:, :, T]))
                        st.wait()
                        v.tensor_tensor_scan(flat(xr), flat(kx), flat(inj), 0.0, ALU.mult, ALU.add).then_inc(q["xr_done"], 1)
                        v.wait_ge(landed[b], i * (T * 16) + T * 16)
                        hold(v)
                        v.wait_ge(q["xr_done"], c(READY))
                        st(v.tensor_tensor(z[:], rows[b][:], turned(xr[:, :, 1:X]), ALU.add))
                        st.wait()
                        st(v.scalar_tensor_tensor(z[:], z[:], SLOPE, z[:], ALU.mult, ALU.max))
                        st.wait()
                        v.tensor_tensor(z[:], z[:], bc(S.att[:, layer * D:(layer + 1) * D], [P, T, D], 1),
                                        ALU.mult).then_inc(q["z_done"], 1)
                        v.wait_ge(q["z_done"], c(READY))
                        st(v.tensor_reduce(score[:, 1:X], z[:], AX, ALU.add))
                    st(v.tensor_copy(score[:, 0:1], mrow[:, T:X]))
                    st.wait()
                    st(v.tensor_tensor_scan(mrow[:], pen, score[:], 0.0, ALU.add, ALU.max))
                    st.wait()
                    st(v.tensor_tensor(e2[:, 0, 1:X], mrow[:, 0:T], pen[:, 1:X], ALU.add))
                    st(v.tensor_copy(e2[:, 1, 0:1], srow[:, T:X]))
                    st.wait()
                    st(v.tensor_tensor(e2[:, 1, 1:X], score[:, 1:X], mrow[:, 1:X], ALU.subtract))
                    st.wait()
                    v.tensor_tensor(e2[:, 0, 1:X], e2[:, 0, 1:X], mrow[:, 1:X], ALU.subtract).then_inc(q["exp_ask"], 1)
                    v.wait_ge(q["exp_ask"], c(READY))
                    hold(v)
                    v.wait_ge(q["exp_done"], c(READY))
                    hold(v)
                    v.tensor_tensor(turned(y[:, :, 1:X]), rows[b][:, :, 0:D], bc(e2[:, 1, 1:X], [P, T, D], 2),
                                    ALU.mult).then_inc(q["y_done"], 1)
                    st(v.tensor_copy(y[:, :, 0], osum[:, :, T]))
                    v.tensor_tensor_scan(srow[:], e2[:, 0, :], e2[:, 1, :], 0.0, ALU.mult, ALU.add).then_inc(q["srow_done"], 1)
                    v.wait_ge(q["srow_done"], c(READY))
                    hold(v)
                    v.wait_ge(kept[b], i * 16 + 16)
                    st(v.tensor_copy(out[b][:, :, D], srow[:, 1:X]))
                    v.tensor_copy(out[b][:, :, D + 1], mrow[:, 1:X]).then_inc(q["out_sm_done"], 1)
                    v.wait_ge(q["dx_done"], c(READY))
                    hold(v)
                    v.wait_ge(q["out_o_done"], c(PREV))
                    hold(v)
                    v.wait_ge(q["y_done"], c(READY))
                    hold(v)
                    v.wait_ge(q["out_sm_done"], c(READY))
                    hold(v)
                    st.wait()
                    v.tensor_tensor_scan(flat(osum), flat(dx), flat(y), 0.0, ALU.mult, ALU.add).then_inc(q["osum_done"], 1)
                    v.wait_ge(q["osum_done"], c(READY))
                    hold(v)
                st.leave(PAIRS)
            st(v.tensor_copy(S.final[:, 0, :], mrow[:, T:X].to_broadcast([P, D])))
            st(v.tensor_copy(S.final[:, 1, :], srow[:, T:X].to_broadcast([P, D])))
            st(v.tensor_copy(S.final[:, 2, :], osum[:, :, T]))
            st.wait()


def carry_phase(nc, S, R, tag, per_feature):
    with nc.cleanup_on_exit(), ExitStack() as ctx:
        sb = lambda n, s: ctx.enter_context(nc.sbuf_tensor(f"{tag}_{n}", s, F32))
        ps = lambda n, s: ctx.enter_context(nc.psum_tensor(f"{tag}_{n}", s, F32))
        sem = lambda n: nc.alloc_semaphore(f"{tag}_{n}")
        W = 2 * D if per_feature else SW
        ft = sb("ft", [D, 3, P])
        carry = sb("carry", [D, 3, P + 1])
        ee = sb("ee", [D, 2, P])
        row, row_m = sb("row", [P, W]), sb("row_m", [P, D])
        state = sb("state", [P, 3, D])
        mx, e2 = sb("mx", [P, D]), sb("e2", [P, 2, D])
        ft_ps, in_ps = ps("ft_ps", [D, 3, P]), ps("in_ps", [P, 3, D])
        names = ["ft_done", "cy_steps", "ee_ask", "ee_done", "carry_done", "in_done", "rows_in", "e2_ask", "e2_done",
                 "mended", "mend_out"]
        q = {n: sem(n) for n in names}
        block = ctx.enter_context(nc.Block())
        table = R.state_so if per_feature else R.state

        @block.gpsimd
        def _(pool):
            at = bass.IndirectOffsetOnAxis(ap=S.head_i[:], axis=0)
            pool.indirect_dma_start(row[:], None, table, at).then_inc(q["rows_in"], 16)
            if per_feature:
                pool.indirect_dma_start(row_m[:], None, R.state_m, at).then_inc(q["rows_in"], 16)
            pool.wait_ge(q["mended"], 1)
            pool.indirect_dma_start(table, bass.IndirectOffsetOnAxis(ap=S.mend_i[:], axis=0), row[:], None
                                    ).then_inc(q["mend_out"], 16)
            pool.wait_ge(q["mend_out"], 16)

        @block.tensor
        def _(pe):
            for n in range(3):
                last = pe.transpose(ft_ps[:, n, :], S.final[:, n, :], S.ident[:])
            last.then_inc(q["ft_done"], 1)
            pe.wait_ge(q["carry_done"], 1)
            for n in range(3):
                last = pe.transpose(in_ps[:, n, :], carry[:, n, 0:P], S.ident[0:D, 0:D])
            last.then_inc(q["in_done"], 1)

        @block.scalar
        def _(act):
            act.wait_ge(q["ee_ask"], 1)
            act.activation(ee[:], ee[:], ACT.Exp).then_inc(q["ee_done"], 1)
            act.wait_ge(q["e2_ask"], 1)
            act.activation(e2[:], e2[:], ACT.Exp).then_inc(q["e2_done"], 1)

        @block.vector
        def _(v):
            st = Steps(v, q["cy_steps"])
            v.wait_ge(q["ft_done"], 1)
            st(v.tensor_copy(ft[:], ft_ps[:]))
            st(v.memset(carry[:, 0, 0:1], -BIG))
            st(v.memset(carry[:, 1:3, 0:1], 0.0))
            st.wait()
            st(v.tensor_tensor_scan(carry[:, 0, 1:P + 1], S.pen_part[:], ft[:, 0, :], -BIG, ALU.add, ALU.max))
            st.wait()
            st(v.tensor_tensor(ee[:, 0, :], carry[:, 0, 0:P], S.pen_part[:], ALU.add))
            st(v.tensor_tensor(ee[:, 1, :], ft[:, 0, :], carry[:, 0, 1:P + 1], ALU.subtract))
            st.wait()
            st(v.tensor_tensor(ee[:, 0, :], ee[:, 0, :], carry[:, 0, 1:P + 1], ALU.subtract))
            st.wait()
            v.sem_inc(q["ee_ask"], 1)
            v.wait_ge(q["ee_done"], 1)
            st(v.tensor_tensor(ft[:, 1:3, :], ft[:, 1:3, :], bc(ee[:, 1, :], [D, 2, P], 1), ALU.mult))
            st.wait()
            st(v.tensor_tensor_scan(carry[:, 1, 1:P + 1], ee[:, 0, :], ft[:, 1, :], 0.0, ALU.mult, ALU.add))
            st(v.tensor_tensor_scan(carry[:, 2, 1:P + 1], ee[:, 0, :], ft[:, 2, :], 0.0, ALU.mult, ALU.add))
            st.wait()
            v.sem_inc(q["carry_done"], 1)
            v.wait_ge(q["rows_in"], 32 if per_feature else 16)
            if per_feature:
                parts = (row_m[:], row[:, 0:D], row[:, D:2 * D])
            else:
                parts = (row[:, D + 1:D + 2].to_broadcast([P, D]), row[:, D:D + 1].to_broadcast([P, D]), row[:, 0:D])
            for n, part in enumerate(parts):
                st(v.tensor_copy(state[:, n, :], part))
            st.wait()
            v.wait_ge(q["in_done"], 1)
            st(v.tensor_tensor(mx[:], state[:, 0, :], in_ps[:, 0, :], ALU.max))
            st.wait()
            st(v.tensor_tensor(e2[:, 0, :], state[:, 0, :], mx[:], ALU.subtract))
            st(v.tensor_tensor(e2[:, 1, :], in_ps[:, 0, :], mx[:], ALU.subtract))
            st.wait()
            v.sem_inc(q["e2_ask"], 1)
            v.wait_ge(q["e2_done"], 1)
            for n in (1, 2):
                st(v.tensor_tensor(state[:, n, :], state[:, n, :], e2[:, 0, :], ALU.mult))
                st(v.tensor_tensor(mx[:] if n == 1 else state[:, 0, :], in_ps[:, n, :], e2[:, 1, :], ALU.mult))
            st.wait()
            if per_feature:
                s_out, s_in, s_add = row[:, 0:D], state[:, 1, :], mx[:]
                o_out = row[:, D:2 * D]
            else:
                s_out, s_in, s_add = row[:, D:D + 1], state[:, 1, 0:1], mx[:, 0:1]
                o_out = row[:, 0:D]
            st(v.tensor_tensor(s_out, s_in, s_add, ALU.add))
            st(v.tensor_tensor(o_out, state[:, 2, :], state[:, 0, :], ALU.add))
            st.wait()
            v.sem_inc(q["mended"], 1)


def nodes_phase(nc, io, S, R, stage):
    tag = f"n{stage}"
    layer = stage - 2
    mid, norm, edge_rows = stage in (2, 3), stage in (0, 1, 4), 1 <= stage <= 3
    W = 2 * D if stage == 1 else SW
    with nc.cleanup_on_exit(), ExitStack() as ctx:
        sb = lambda n, s: ctx.enter_context(nc.sbuf_tensor(f"{tag}_{n}", s, F32))
        sem = lambda n: nc.alloc_semaphore(f"{tag}_{n}")
        node_state = sb("state", [P, KN, W]) if stage else None
        part = None if stage else [sb(f"part{k}", [P, KN, SW]) for k in range(TABLES)]
        new, sq = sb("new", [P, KN, D]), sb("sq", [P, KN, D])
        stat, root = sb("stat", [P, KN]), sb("root", [P, KN])
        rec = sb("rec", [P, KN, D]) if stage == 1 else sb("rec", [P, KN])
        first = Linear(ctx, nc, tag + "a", D) if stage == 1 else None
        ahead = Linear(ctx, nc, tag + "b", 2 * D if edge_rows else D) if 1 <= stage <= 4 else None
        lr = sb("lr", [P, KN, 2 * D]) if edge_rows else None
        t3 = sb("t3", [P, KN, SW]) if stage == 4 else None
        q = {n: sem(n) for n in ("steps", "new_done", "gelu_done", "centred", "sq_done", "var_done", "root_done",
                                 "scaled", "relu_done", "t3_done", "stored", "inject", "head")}
        nodes_in = [sem(f"nodes_in{g}") for g in range(len(NODE_GROUPS))]
        block = ctx.enter_context(nc.Block())
        state_table = R.state_so if stage == 1 else R.state
        row_done = ahead.taken if edge_rows else q["relu_done"] if stage == 0 else q["t3_done"]
        cut = lambda t, g: t[:, NODE_GROUPS[g][0]:sum(NODE_GROUPS[g])]

        @block.sync
        def _(sp):
            if stage == 0:
                for g in range(len(NODE_GROUPS)):
                    for k in range(TABLES):
                        sp.dma_start(cut(part[k], g), cut(node_rows(R.acc[k][0:NODES]), g)).then_inc(nodes_in[g], 16)
            for g in range(len(NODE_GROUPS)):
                if stage == 0:
                    sp.wait_ge(row_done, g + 1)
                    sp.dma_start(cut(node_rows(R.table), g), cut(S.h, g)).then_inc(q["stored"], 16)
                elif edge_rows:
                    sp.wait_ge(row_done, g + 1)
                    sp.dma_start(cut(node_rows(R.table), g), cut(lr, g)[:, :, 0:D]).then_inc(q["stored"], 16)
                    sp.dma_start(cut(node_rows(R.table_r), g), cut(lr, g)[:, :, D:2 * D]).then_inc(q["stored"], 16)
                elif stage == 4:
                    sp.wait_ge(row_done, g + 1)
                    sp.dma_start(cut(node_rows(R.table3), g), cut(t3, g)).then_inc(q["stored"], 16)
                else:
                    sp.wait_ge(q["new_done"], g + 1)
                    sp.dma_start(cut(io["out"].rearrange("p (k f) -> p k f", f=D), g), cut(new, g)).then_inc(q["stored"], 16)
            sp.wait_ge(q["stored"], 16 * len(NODE_GROUPS) * (2 if edge_rows else 1))

        @block.gpsimd
        def _(pool):
            if stage == 0:
                return
            for g, (k0, n) in enumerate(NODE_GROUPS):
                for k in range(k0, k0 + n):
                    pool.indirect_dma_start(node_state[:, k, :], None, state_table,
                                            bass.IndirectOffsetOnAxis(ap=S.end_i[:, k:k + 1], axis=0)
                                            ).then_inc(nodes_in[g], 16)
            if stage == 5:
                for g, (k0, n) in enumerate(NODE_GROUPS):
                    pool.wait_ge(nodes_in[g], 16 * n)
                return
            for g, (k0, n) in enumerate(NODE_GROUPS):
                pool.wait_ge(row_done, g + 1)
                for k in range(k0, k0 + n):
                    at = bass.IndirectOffsetOnAxis(ap=S.start_i[:, k:k + 1], axis=0)
                    if edge_rows:
                        pool.indirect_dma_start(R.inject, at, lr[:, k, D:2 * D], None).then_inc(q["inject"], 16)
                    else:
                        pool.indirect_dma_start(R.inject1, at, t3[:, k, D + 1:D + 2], None).then_inc(q["inject"], 16)
            pool.wait_ge(q["stored"], 16 * len(NODE_GROUPS) * (2 if edge_rows else 1))
            at = bass.IndirectOffsetOnAxis(ap=S.dst0[:], axis=0)
            if edge_rows:
                pool.indirect_dma_start(S.head_row[:, 0:D], None, R.table_r, at).then_inc(q["head"], 16)
            else:
                pool.indirect_dma_start(S.head_row[:], None, R.table3, at).then_inc(q["head"], 16)
            pool.wait_ge(q["inject"], 16 * KN)
            pool.wait_ge(q["head"], 16)

        @block.tensor
        def _(pe):
            ident, ones = S.ident[:], S.ones[0:1, :]
            if stage == 1:
                w_ahead, bias = S.wlr[:, 0, :], S.blr[0:1, 0:2 * D]
            elif mid:
                w_ahead, bias = S.wlr[:, layer + 1, :], S.blr[0:1, (layer + 1) * 2 * D:(layer + 2) * 2 * D]
            else:
                w_ahead, bias = S.w3[:], None
            turn1 = lambda g: first.turn(pe, g, new, q["new_done"], ident)
            mul1 = lambda g: first.multiply(pe, g, S.w1[:], S.b1[0:1, :], ones)
            turn2 = lambda g: ahead.turn(pe, g, S.h if norm else new, q["relu_done"] if norm else q["gelu_done"], ident)
            mul2 = lambda g: ahead.multiply(pe, g, w_ahead, bias, ones)
            if stage == 1:
                skewed([(turn2, 5), (turn1, 0), (mul2, 6), (mul1, 1)])
            elif stage == 4:
                skewed([(turn2, 5), (mul2, 6)])
            elif mid:
                skewed([(turn2, 0), (mul2, 0)])

        @block.scalar
        def _(act):
            def gelu(g):
                act.wait_ge(q["new_done"], g + 1)
                act.activation(cut(new, g), cut(new, g), ACT.Gelu).then_inc(q["gelu_done"], 1)

            def square(g):
                act.wait_ge(q["centred"], g + 1)
                act.activation(cut(sq, g), cut(S.h, g), ACT.Square).then_inc(q["sq_done"], 1)

            def sqrt(g):
                act.wait_ge(q["var_done"], g + 1)
                act.activation(cut(root, g), cut(stat, g), ACT.Sqrt).then_inc(q["root_done"], 1)

            def relu(g):
                act.wait_ge(q["scaled"], g + 1)
                act.activation(cut(S.h, g), cut(S.h, g), ACT.Relu).then_inc(q["relu_done"], 1)

            copy1, take1 = (lambda g: first.copy(act, g)), (lambda g: first.take(act, g, new, ACT.Relu))
            copy2 = lambda g: ahead.copy(act, g)
            take2 = lambda g: ahead.take(act, g, lr if edge_rows else t3[:, :, 0:D], ACT.Copy)
            if stage == 0:
                skewed([(relu, 3), (sqrt, 2), (square, 1)])
            elif stage == 1:
                skewed([(relu, 4), (take2, 6), (take1, 1), (copy2, 5), (sqrt, 3), (copy1, 0), (square, 2)])
            elif stage == 4:
                skewed([(relu, 4), (take2, 6), (copy2, 5), (sqrt, 3), (gelu, 0), (square, 2)])
            elif mid:
                skewed([(gelu, 0), (copy2, 0), (take2, 0)])

        @block.vector
        def _(v):
            st = Steps(v, q["steps"])

            def output(g):
                k0, n = NODE_GROUPS[g]
                state, shape = cut(node_state, g) if stage else None, [P, n, D]
                if stage == 0:
                    v.wait_ge(nodes_in[g], 16 * TABLES)
                    for k in range(1, TABLES):
                        st(v.tensor_tensor(cut(part[0], g), cut(part[0], g), cut(part[k], g), ALU.add))
                        st.wait()
                    st(v.tensor_scalar(cut(rec, g), cut(part[0], g)[:, :, D], 1.2e-38, None, ALU.max))
                    st.wait()
                    st(v.reciprocal(cut(rec, g), cut(rec, g)))
                    st.wait()
                    v.tensor_tensor(cut(new, g), cut(part[0], g)[:, :, 0:D], bc(cut(rec, g), shape, 2),
                                    ALU.mult).then_inc(q["new_done"], 1)
                    return
                v.wait_ge(nodes_in[g], 16 * n)
                if stage == 1:
                    st(v.tensor_scalar(cut(rec, g), state[:, :, 0:D], 1.2e-38, None, ALU.max))
                    st.wait()
                    st(v.reciprocal(cut(rec, g), cut(rec, g)))
                    st.wait()
                    v.tensor_tensor(cut(new, g), state[:, :, D:2 * D], cut(rec, g), ALU.mult).then_inc(q["new_done"], 1)
                    return
                if stage == 5:
                    st(v.tensor_scalar(cut(rec, g), state[:, :, D], 1e-16, None, ALU.add))
                    st.wait()
                    st(v.reciprocal(cut(rec, g), cut(rec, g)))
                else:
                    st(v.reciprocal(cut(rec, g), state[:, :, D]))
                st.wait()
                st(v.tensor_tensor(cut(new, g), state[:, :, 0:D], bc(cut(rec, g), shape, 2), ALU.mult))
                st.wait()
                bias = S.bias3[:] if stage == 5 else S.bias2[:, layer * D:(layer + 1) * D]
                if stage == 5:
                    st(v.tensor_tensor(cut(new, g), cut(new, g), bc(bias, shape, 1), ALU.add))
                    st.wait()
                    v.tensor_tensor(cut(new, g), cut(new, g), cut(S.xres, g), ALU.add).then_inc(q["new_done"], 1)
                else:
                    v.tensor_tensor(cut(new, g), cut(new, g), bc(bias, shape, 1), ALU.add).then_inc(q["new_done"], 1)

            def centre(g):
                k0, n = NODE_GROUPS[g]
                v.wait_ge((q["new_done"], first and first.taken, 0, 0, q["gelu_done"])[stage], g + 1)
                st(v.tensor_tensor(cut(S.xres, g), cut(S.xres, g), cut(new, g), ALU.add))
                st.wait()
                st(v.tensor_reduce(cut(stat, g), cut(S.xres, g), AX, ALU.add))
                st.wait()
                st(v.tensor_scalar(cut(stat, g), cut(stat, g), -1.0 / D, None, ALU.mult))
                st.wait()
                v.tensor_tensor(cut(S.h, g), cut(S.xres, g), bc(cut(stat, g), [P, n, D], 2),
                                ALU.add).then_inc(q["centred"], 1)

            def variance(g):
                v.wait_ge(q["sq_done"], g + 1)
                v.wait_ge(q["centred"], g + 1)
                st(v.tensor_reduce(cut(stat, g), cut(sq, g), AX, ALU.add))
                st.wait()
                v.tensor_scalar(cut(stat, g), cut(stat, g), 1.0 / D, EPS, ALU.mult, ALU.add).then_inc(q["var_done"], 1)

            def scale(g):
                k0, n = NODE_GROUPS[g]
                v.wait_ge(q["root_done"], g + 1)
                st(v.reciprocal(cut(root, g), cut(root, g)))
                st.wait()
                v.tensor_tensor(cut(S.h, g), cut(S.h, g), bc(cut(root, g), [P, n, D], 2), ALU.mult).then_inc(q["scaled"], 1)

            def scores(g):
                k0, n = NODE_GROUPS[g]
                v.wait_ge(ahead.taken, g + 1)
                for col, at in ((D, D + DE), (D + 1, 0)):
                    st(v.tensor_tensor(cut(sq, g), cut(t3, g)[:, :, 0:D], bc(S.wa[:, at:at + D], [P, n, D], 1), ALU.mult))
                    st.wait()
                    last = v.tensor_reduce(cut(t3, g)[:, :, col], cut(sq, g), AX, ALU.add)
                    if col == D:
                        st(last)
                        st.wait()
                last.then_inc(q["t3_done"], 1)

            if stage == 0:
                skewed([(scale, 3), (variance, 2), (output, 0), (centre, 1)])
                v.wait_ge(q["relu_done"], len(NODE_GROUPS))
                st(v.tensor_tensor(S.xres[:], S.xres[:], S.h[:], ALU.add))
                st.wait()
            elif stage == 1:
                skewed([(scale, 4), (output, 0), (variance, 3), (centre, 2)])
            elif stage == 4:
                skewed([(scale, 4), (output, 0), (variance, 3), (centre, 2), (scores, 7)])
            else:
                skewed([(output, 0)])


def build_program(nc, io):
    with ExitStack() as ctx:
        S, R = Scratch(), Scratch()
        sb = lambda n, s, d=F32: ctx.enter_context(nc.sbuf_tensor(n, s, d))
        dram = lambda n, s, d=F32: nc.dram_tensor(n, s, d, kind="Internal").ap()
        S.pen = sb("pen", [P, CHUNKS * X])
        S.keep = sb("keep", [P, CHUNKS * X])
        S.xres = sb("xres", [P, KN, D])
        S.h = sb("h", [P, KN, D])
        S.ident, S.upto, S.ones = sb("ident", [P, P]), sb("upto", [P, P]), sb("ones", [P, P])
        S.w1, S.w3, S.wlr = sb("w1", [D, D]), sb("w3", [D, D]), sb("wlr", [D, LAYERS, 2 * D])
        S.b1, S.bias3, S.wa = sb("b1", [P, D]), sb("bias3", [P, D]), sb("wa", [P, 2 * D + DE])
        S.blr, S.att, S.bias2 = sb("blr", [P, LAYERS * 2 * D]), sb("att", [P, LAYERS * D]), sb("bias2", [P, LAYERS * D])
        S.pf, S.node_dump, S.edge_dump = sb("pf", [P, 1]), sb("node_dump", [P, 1]), sb("edge_dump", [P, 1])
        S.part_end, S.any_start = sb("part_end", [P, 1]), sb("any_start", [P, 1])
        S.node_skip = sb("node_skip", [P, KN])
        S.count = sb("count", [P, KN])
        S.end_i, S.start_i = sb("end_i", [P, KN], I32), sb("start_i", [P, KN], I32)
        S.dst0, S.head_i, S.mend_i = sb("dst0", [P, 1], I32), sb("head_i", [P, 1], I32), sb("mend_i", [P, 1], I32)
        S.pen_part = sb("pen_part", [D, P])
        S.head_row = sb("head_row", [P, SW])
        S.final = sb("final", [P, 3, D])
        R.acc = [dram(f"acc{k}", (ACC_ROWS, SW)) for k in range(TABLES)]
        R.inject, R.inject1 = dram("inject", (ROWS + NODES, D)), dram("inject1", (ROWS + NODES, 1))
        R.seg_info, R.last_edge = dram("seg_info", (3, NODES), I32), dram("last_edge", (NODES, 1), I32)
        R.table, R.table_r, R.table3 = dram("table", (NODES, D)), dram("table_r", (NODES, D)), dram("table3", (NODES, SW))
        R.state_so, R.state_m, R.state = dram("state_so", (EMPTY + 1, 2 * D)), dram("state_m", (ROWS, D)), dram("state", (EMPTY + 1, SW))

        with ExitStack() as early:
            sbe = lambda n, s, d=F32: early.enter_context(nc.sbuf_tensor(n, s, d))
            S.src_i, S.dst_i = sbe("src_i", [P, TILES], I32), sbe("dst_i", [P, TILES], I32)
            S.ew = sbe("ew", [P, TILES])
            S.prev_i = sbe("prev_i", [P, TILES], I32)
            S.lower, S.col16 = sbe("lower", [P, P]), sbe("col16", [P, P], BF16)
            S.zeros = sbe("zeros", [P, ACC_ROWS // P * SW])
            setup_phase(nc, io, S)
            aggregate_phase(nc, io, S, R)
        nodes_phase(nc, io, S, R, 0)
        feature_softmax_phase(nc, io, S, R)
        carry_phase(nc, S, R, "c1", True)
        nodes_phase(nc, io, S, R, 1)
        for layer in range(LAYERS + 1):
            scalar_softmax_phase(nc, io, S, R, layer)
            carry_phase(nc, S, R, f"c{layer + 2}", False)
            nodes_phase(nc, io, S, R, layer + 2)


def laid_out(x, src, dst, edge_attr_16, edge_attr_64, edge_weight1, L1_gnn_W, L1_gnn_b, L2_gnn_Wl, L2_gnn_bl,
             L2_gnn_Wr, L2_gnn_br, L2_gnn_att, L2_gnn_bias, L3_gnn_W, L3_gnn_w_att, L3_gnn_bias):
    import numpy as np

    def rows(a, n, fill=0):
        a = np.asarray(a)
        return np.concatenate([a, np.full((n - a.shape[0],) + a.shape[1:], fill, a.dtype)])

    out = {
        "x": rows(x, NODES).reshape(P, KN * D),
        "src": rows(src, ROWS, NODES - 1).reshape(P, TILES),
        "dst": np.concatenate([np.full(1, -1, np.asarray(dst).dtype), rows(dst, ROWS, NODES - 1)]),
        "edge_w": rows(np.asarray(edge_weight1).reshape(-1), ROWS).reshape(P, TILES),
        "ea64": rows(edge_attr_64, ROWS),
        "ea16": rows(edge_attr_16, ROWS),
        "w1t": np.asarray(L1_gnn_W).T,
        "b1": np.asarray(L1_gnn_b).reshape(1, D),
        "wlr": np.concatenate([np.asarray(L2_gnn_Wl), np.asarray(L2_gnn_Wr)], axis=2),
        "blr": np.concatenate([np.asarray(L2_gnn_bl), np.asarray(L2_gnn_br)], axis=1).reshape(1, -1),
        "att": np.asarray(L2_gnn_att).reshape(1, -1),
        "bias2": np.asarray(L2_gnn_bias).reshape(1, -1),
        "w3": np.asarray(L3_gnn_W),
        "wa": np.asarray(L3_gnn_w_att).reshape(1, -1),
        "bias3": np.asarray(L3_gnn_bias).reshape(1, D),
    }
    return {k: np.ascontiguousarray(a) for k, a in out.items()}


def kernel(**inputs):
    import numpy as np
    import concourse.bacc as bacc
    from concourse.bass_utils import run_bass_kernel_spmd

    nc = bacc.Bacc("TRN2", target_bir_lowering=False, num_devices=1)
    arrays, io = {}, {}
    for name, a in laid_out(**inputs).items():
        arrays[f"in_{name}"] = a
        io[name] = nc.dram_tensor(f"in_{name}", a.shape, mybir.dt.from_np(a.dtype), kind="ExternalInput").ap()
    io["out"] = nc.dram_tensor("out_nodes", (P, KN * D), F32, kind="ExternalOutput").ap()
    build_program(nc, io)
    result = run_bass_kernel_spmd(nc, [arrays], core_ids=[0])
    return np.ascontiguousarray(result.results[0]["out_nodes"].reshape(NODES, D)[:N])
```

```python
from contextlib import ExitStack

import concourse.bass as bass
from concourse import mybir

ALU = mybir.AluOpType
ACT = mybir.ActivationFunctionType
AX = mybir.AxisListType.X
F32 = mybir.dt.float32
BF16 = mybir.dt.bfloat16
I32 = mybir.dt.int32

P = 128
N = 6250
D = 64
DE = 16
E = 206250
LAYERS = 3
KN = -(-N // P)
NODES = P * KN
TILES = -(-E // P)
ROWS = P * TILES
T = 26
CHUNKS = TILES // T
PAIRS = CHUNKS // 2
X = T + 1
G = 2
GROUPS = T // G
PARTS = ((0, GROUPS // 2 + 1), (GROUPS // 2 + 1, GROUPS))
HALF = T // 2
TABLES = 4
SW = D + 2
EMPTY = ROWS + P
ACC_ROWS = NODES + P
BIG = 1.0e38
SLOPE = 0.2
EPS = 1e-5
assert TILES % (2 * T) == 0 and (2 * T) % TABLES == 0 and T % G == 0

CREDIT = 2
READY, PREV, FREE = 1 + CREDIT, CREDIT, CREDIT - 1


class Steps:

    def __init__(self, eng, sem):
        self.eng, self.sem, self.done, self.turn, self.per_turn, self.n = eng, sem, 0, None, 0, 0

    def __call__(self, ins):
        ins.then_inc(self.sem, 1)
        self.n += 1

    def wait(self):
        if self.turn is None:
            self.eng.wait_ge(self.sem, self.done + self.n)
        else:
            self.eng.wait_ge(self.sem, self.turn * self.per_turn + (self.done + self.n))

    def enter(self, turn, per_turn):
        self.done, self.n, self.turn, self.per_turn = self.done + self.n, 0, turn, per_turn

    def leave(self, turns):
        assert self.n == self.per_turn, (self.n, self.per_turn)
        self.done, self.n, self.turn = self.done + self.n * turns, 0, None


def hold(eng):
    eng.nop(nofuse=True)


def bc(ap, shape, axis):
    return ap.unsqueeze(axis).to_broadcast(shape)


def turned(ap):
    return ap.rearrange("p a b -> p b a")


def setup_phase(nc, io, S):
    with nc.cleanup_on_exit(), ExitStack() as ctx:
        sb = lambda n, s, d: ctx.enter_context(nc.sbuf_tensor(n, s, d))
        sem = lambda n: nc.alloc_semaphore(n)
        jrow = sb("jrow", [P, P], I32)
        pcol = sb("pcol", [P, 1], I32)
        node_no = sb("node_no", [P, KN], I32)
        jf = sb("jf", [P, P], F32)
        weights_in, edges_in, iotas, steps = sem("weights_in"), sem("edges_in"), sem("iotas"), sem("setup_steps")
        exp_done = sem("exp_done")
        block = ctx.enter_context(nc.Block())

        @block.sync
        def _(sp):
            sp.dma_start(S.exp_w[:], io["edge_w"]).then_inc(weights_in, 16)
            sp.dma_start(S.src_i[:], io["src"]).then_inc(edges_in, 16)
            sp.dma_start(S.dst_i[:], io["dst"][1:ROWS + 1].rearrange("(p t) -> p t", p=P)).then_inc(edges_in, 16)
            sp.wait_ge(edges_in, 32)

        @block.scalar
        def _(act):
            act.wait_ge(weights_in, 16)
            act.activation(S.exp_w[:], S.exp_w[:], ACT.Exp).then_inc(exp_done, 1)
            act.wait_ge(exp_done, 1)

        @block.gpsimd
        def _(pool):
            pool.iota(jrow[:], [[1, P]], 0, 0).then_inc(iotas, 1)
            pool.iota(pcol[:], [[0, 1]], 0, 1).then_inc(iotas, 1)
            pool.iota(node_no[:], [[1, KN]], ROWS, KN).then_inc(iotas, 1)

        @block.vector
        def _(v):
            st = Steps(v, steps)
            v.wait_ge(iotas, 3)
            st(v.tensor_copy(jf[:], jrow[:]))
            st(v.tensor_copy(S.pf[:], pcol[:]))
            st(v.tensor_copy(S.node_skip[:], node_no[:]))
            st(v.memset(S.ones[:], 1.0))
            st(v.memset(S.zeros[:], 0.0))
            st.wait()
            st(v.tensor_copy(S.col16[:], jf[:]))
            st(v.tensor_scalar(S.ident[:], jf[:], S.pf[:], None, ALU.is_equal))
            st(v.tensor_scalar(S.lower[:], jf[:], S.pf[:], None, ALU.is_lt))
            st(v.tensor_scalar(S.upto[:], jf[:], S.pf[:], None, ALU.is_ge))
            st(v.tensor_scalar(S.node_dump[:], S.pf[:], float(NODES), None, ALU.add))
            st(v.tensor_scalar(S.edge_dump[:], S.pf[:], float(ROWS), None, ALU.add))
            st(v.tensor_scalar(S.part_end[:], S.pf[:], float(TILES), float(TILES), ALU.mult, ALU.add))
            v.wait_ge(edges_in, 32)
            st(v.tensor_copy(S.dst0[:], S.dst_i[:, 0:1]))
            st.wait()


def aggregate_phase(nc, io, S, R):
    with nc.cleanup_on_exit(), ExitStack() as ctx:
        sb = lambda n, s, d: ctx.enter_context(nc.sbuf_tensor(n, s, d))
        ps = lambda n, s: ctx.enter_context(nc.psum_tensor(n, s, F32))
        sem = lambda n: nc.alloc_semaphore(n)
        part_i = sb("part_i", [P, 2, T], I32)
        part16 = sb("part16", [P, 2, T], BF16)
        dst_f, prev_f = sb("dst_f", [P, TILES], F32), sb("prev_f", [P, TILES], F32)
        ef = [sb(f"ef{b}", [P, T, D], F32) for b in range(2)]
        msg = [sb(f"msg{b}", [P, T, SW], F32) for b in range(2)]
        total = [sb(f"total{b}", [P, T, SW], F32) for b in range(2)]
        srcs = [sb(f"srcs{b}", [P, T], F32) for b in range(2)]
        lo1h = [sb(f"lo1h{b}", [P, T, P], BF16) for b in range(2)]
        hi1h = [sb(f"hi1h{b}", [P, T, KN], BF16) for b in range(2)]
        eq = [sb(f"eq{b}", [P, G, P], F32) for b in range(2)]
        earlier = [sb(f"earlier{b}", [P, G, P], F32) for b in range(2)]
        rank = sb("rank", [P, T], F32)
        target = sb("target", [P, T], F32)
        rows_i = [sb(f"rows_i{b}", [P, T], I32) for b in range(2)]
        row_of = [ps(f"row_of{b}", [P, G, P]) for b in range(2)]
        summed = [ps(f"summed{b}", [P, G, SW]) for b in range(2)]
        hist = ps("hist", [P, KN])
        prefix, seg_ps, s_ps = ps("prefix", [P, 2, KN]), ps("seg_ps", [KN, 3, P]), ps("s_ps", [D, P])
        tot, incl, tmp, last = [sb(f"seg_{n}", [P, KN], F32) for n in ("tot", "incl", "tmp", "last")]
        seg, segn = sb("seg", [P, 3, KN], F32), sb("segn", [P, 3, KN], F32)
        segt, segn_i = sb("segt", [KN, 3, P], I32), sb("segn_i", [P, 3, KN], I32)
        eh_f, cond = sb("eh_f", [P, 1], F32), sb("cond", [P, 1], F32)
        ef_in = [sem(f"ef_in{b}") for b in range(2)]
        names = ["loaded", "msg_done", "srcs_done", "onehot_done", "weight_done", "row_of_done",
                 "eq_done", "earlier_done", "summed_done", "total_done", "rows_done", "scattered", "zeroed",
                 "agg_steps", "hist_done", "hist_kept", "any_done", "counted", "prefix_done",
                 "seg_ready", "seg_turned", "segt_ready", "seg_out", "seg_back", "heads_in"]
        q = {n: sem(n) for n in names}
        acc_done = [sem(f"acc_done{k}") for k in range(TABLES)]
        dump_rows = (R.state, R.state_so)
        n_loads = 9
        block = ctx.enter_context(nc.Block())

        @block.sync
        def _(sp):
            feats = io["ea64"].rearrange("(p t) f -> p (t f)", p=P)
            inj = R.inject[0:ROWS].rearrange("(p t) f -> p (t f)", p=P)
            with sp.Fori(0, PAIRS) as i:
                for b in range(2):
                    sp.wait_ge(q["msg_done"], i * 2 + (b + FREE))
                    hold(sp)
                    for half in range(2):
                        at = half * HALF * D
                        sp.wait_ge(q["summed_done"], i * (2 * GROUPS) + (b * GROUPS + half * GROUPS // 2 + 4))
                        sp.dma_start(ef[b][:].rearrange("p t f -> p (t f)")[:, at:at + HALF * D],
                                     feats[:, bass.ds(i * (2 * T * D) + (b * T * D + at), HALF * D)]).then_inc(ef_in[b], 16)
                        sp.wait_ge(q["summed_done"], i * (2 * GROUPS) + (b * GROUPS + half * GROUPS // 2 + 7))
                        sp.dma_start(inj[:, bass.ds(i * (2 * T * D) + (b * T * D + at), HALF * D)],
                                     S.zeros[:, 0:HALF * D]).then_inc(q["zeroed"], 16)
            loads = [
                (S.prev_i[:], io["dst"][0:ROWS].rearrange("(p t) -> p t", p=P)),
                (S.xres[:], io["x"].rearrange("p (k f) -> p k f", f=D)),
                (S.w1[:], io["w1t"]),
                (S.wlr[:], io["wlr"].rearrange("l k m -> k l m")),
                (S.w3[:], io["w3"]),
                (S.att[:], io["att"].to_broadcast([P, LAYERS * D])),
                (S.bias2[:], io["bias2"].to_broadcast([P, LAYERS * D])),
                (S.wa[:], io["wa"].to_broadcast([P, 2 * D + DE])),
                (S.bias3[:], io["bias3"].to_broadcast([P, D])),
            ]
            assert len(loads) == n_loads
            for dst, src in loads:
                sp.dma_start(dst, src).then_inc(q["loaded"], 16)
            sp.dma_start(R.inject1[0:ROWS].rearrange("(p t) f -> p (t f)", p=P),
                         S.zeros[:, 0:TILES]).then_inc(q["zeroed"], 16)
            for table in dump_rows:
                sp.dma_start(table[ROWS:ROWS + P], S.zeros[:, 0:table.shape[1]]).then_inc(q["zeroed"], 16)
            sp.dma_start(R.state[EMPTY:EMPTY + 1, 0:D], S.zeros[0:1, 0:D]).then_inc(q["zeroed"], 16)
            sp.dma_start(R.state[EMPTY:EMPTY + 1, D:SW], S.ones[0:1, 0:2]).then_inc(q["zeroed"], 16)
            sp.dma_start(R.state_so[EMPTY:EMPTY + 1, 0:D], S.ones[0:1, 0:D]).then_inc(q["zeroed"], 16)
            sp.dma_start(R.state_so[EMPTY:EMPTY + 1, D:2 * D], S.zeros[0:1, 0:D]).then_inc(q["zeroed"], 16)
            sp.wait_ge(q["segt_ready"], 1)
            sp.dma_start(R.seg_info.rearrange("s (q r) -> q s r", r=P), segt[:]).then_inc(q["seg_out"], 16)
            sp.dma_start(R.last_edge.rearrange("(q r) one -> q (r one)", r=P), segt[:, 0, :]).then_inc(q["seg_out"], 16)
            sp.wait_ge(q["seg_out"], 32)
            sp.dma_start(segn_i[:], R.seg_info.rearrange("s (p k) -> p s k", k=KN)).then_inc(q["seg_back"], 16)
            sp.wait_ge(q["loaded"], 16 * n_loads)
            sp.wait_ge(q["zeroed"], 16 * (2 * CHUNKS + 5 + len(dump_rows)))

        @block.gpsimd
        def _(pool):
            for k in range(TABLES):
                pool.dma_start(R.acc[k].rearrange("(p r) w -> p (r w)", p=P),
                               S.zeros[:, 0:ACC_ROWS // P * SW]).then_inc(acc_done[k], 16)
            pool.sem_inc(q["scattered"], 1)
            with pool.Fori(0, PAIRS) as i:
                for b in range(2):
                    for t in range(T):
                        for part, (g0, g1) in enumerate(PARTS):
                            if t == G * g0:
                                pool.wait_ge(q["rows_done"], i * 4 + (2 * b + part + READY))
                                hold(pool)
                                pool.wait_ge(q["total_done"], i * (2 * GROUPS) + (b * GROUPS + g1 + CREDIT))
                                hold(pool)
                        g = b * T + t
                        k = g % TABLES
                        pool.wait_ge(acc_done[k], i * (2 * T // TABLES * 16) + (g // TABLES + 1) * 16)
                        hold(pool)
                        if t == TABLES:
                            pool.sem_inc(q["scattered"], 1)
                        pool.indirect_dma_start(
                            R.acc[k], bass.IndirectOffsetOnAxis(ap=rows_i[b][:, t:t + 1], axis=0),
                            total[b][:, t, :], None, compute_op=ALU.add).then_inc(acc_done[k], 16)
            pool.wait_ge(q["seg_out"], 32)
            pool.indirect_dma_start(S.head_i[:], None, R.last_edge,
                                    bass.IndirectOffsetOnAxis(ap=S.dst0[:], axis=0)).then_inc(q["heads_in"], 16)
            for k in range(TABLES):
                pool.wait_ge(acc_done[k], 16 * (1 + TILES // TABLES))

        @block.scalar
        def _(act):
            act.sem_inc(q["weight_done"], CREDIT)
            act.sem_inc(q["total_done"], CREDIT)
            with act.Fori(0, PAIRS) as i:
                for b in range(2):
                    act.wait_ge(q["summed_done"], i * (2 * GROUPS) + (b * GROUPS + 1))
                    hold(act)
                    act.activation(msg[b][:, :, D:D + 1],
                                   bc(S.exp_w[:, bass.ds(i * (2 * T) + b * T, T)], [P, T, 1], 2),
                                   ACT.Copy).then_inc(q["weight_done"], 1)
                    for g in range(GROUPS):
                        at = b * GROUPS + g
                        act.wait_ge(q["summed_done"], i * (2 * GROUPS) + (at + GROUPS + 2))
                        if g == 0:
                            hold(act)
                            act.wait_ge(q["scattered"], i * 2 + (b + 1))
                        act.activation(total[b][:, G * g:G * g + G, :], summed[at % 2][:],
                                       ACT.Copy).then_inc(q["total_done"], 1)
            act.wait_ge(q["hist_done"], 1)
            act.activation(S.count[:], hist[:], ACT.Copy).then_inc(q["hist_kept"], 1)
            act.wait_ge(q["hist_kept"], 1)

        @block.tensor
        def _(pe):
            pe.sem_inc(q["summed_done"], GROUPS + 1)
            pe.sem_inc(q["row_of_done"], CREDIT)
            pe.sem_inc(q["counted"], CREDIT)
            pe.matmul(hist[:], S.zeros[:, 0:P], S.zeros[:, 0:KN], start=True, stop=False,
                      skip_group_check=True)
            with pe.Fori(0, PAIRS) as i:
                for b in range(2):
                    pe.wait_ge(q["srcs_done"], i * 2 + (b + READY))
                    hold(pe)

                    def row_of_group(g):
                        at = b * GROUPS + g
                        pe.wait_ge(q["eq_done"], i * (2 * GROUPS) + (at + FREE))
                        for j in range(G):
                            t = G * g + j
                            last = pe.transpose(row_of[at % 2][:, j, :],
                                                srcs[b][:, t:t + 1].to_broadcast([P, P]), S.ident[:])
                        last.then_inc(q["row_of_done"], 1)

                    row_of_group(0)
                    for g in range(GROUPS):
                        at = b * GROUPS + g
                        if g + 1 < GROUPS:
                            row_of_group(g + 1)
                        if g == 0:
                            pe.wait_ge(q["msg_done"], i * 2 + (b + READY))
                            hold(pe)
                            pe.wait_ge(q["weight_done"], i * 2 + (b + READY))
                            hold(pe)
                        pe.wait_ge(q["total_done"], i * (2 * GROUPS) + (at + FREE))
                        hold(pe)
                        pe.wait_ge(q["eq_done"], i * (2 * GROUPS) + (at + READY))
                        for j in range(G):
                            t = G * g + j
                            last = pe.matmul(summed[at % 2][:, j, :], eq[at % 2][:, j, :],
                                             msg[b][:, t, :], start=True, stop=True,
                                             skip_group_check=True)
                        last.then_inc(q["summed_done"], 1)
                    pe.wait_ge(q["onehot_done"], i * 2 + (b + READY))
                    hold(pe)
                    for t in range(T):
                        last = pe.matmul(hist[:], lo1h[b][:, t, :], hi1h[b][:, t, :], start=False,
                                         stop=False, skip_group_check=True)
                    last.then_inc(q["counted"], 1)
            pe.matmul(hist[:], S.zeros[:, 0:P], S.zeros[:, 0:KN], start=False, stop=True,
                      skip_group_check=True).then_inc(q["hist_done"], 1)
            pe.wait_ge(q["hist_kept"], 1)
            pe.matmul(prefix[:, 0, :], S.upto[:], S.count[:], start=True, stop=True, skip_group_check=True)
            pe.matmul(prefix[:, 1, :], S.ones[:], S.count[:], start=True, stop=True,
                      skip_group_check=True).then_inc(q["prefix_done"], 1)
            pe.wait_ge(q["any_done"], 1)
            pe.transpose(s_ps[:], S.any_start[:].to_broadcast([P, D]), S.ident[:]).then_inc(q["prefix_done"], 1)
            pe.wait_ge(q["seg_ready"], 1)
            for s in range(3):
                last = pe.transpose(seg_ps[:, s, :], seg[:, s, :], S.ident[:])
            last.then_inc(q["seg_turned"], 1)

        def segments(v, st):
            v.wait_ge(q["prefix_done"], 2)
            st(v.tensor_scalar(S.pen_part[:], s_ps[:], -BIG, None, ALU.mult))
            st(v.tensor_copy(tot[:], prefix[:, 1, :]))
            st.wait()
            st(v.tensor_tensor_scan(incl[:], S.ones[:, 0:KN], tot[:], 0.0, ALU.mult, ALU.add))
            st.wait()
            st(v.tensor_tensor(incl[:], incl[:], tot[:], ALU.subtract))
            st.wait()
            st(v.tensor_tensor(tot[:], prefix[:, 0, :], incl[:], ALU.add))
            st.wait()
            st(v.tensor_scalar(seg[:, 0, :], tot[:], -1.0, 0.0, ALU.add, ALU.max))
            st(v.tensor_tensor(seg[:, 1, :], tot[:], S.count[:], ALU.subtract))
            st(v.tensor_copy(seg[:, 2, :], S.count[:]))
            st.wait()
            v.sem_inc(q["seg_ready"], 1)
            v.wait_ge(q["seg_turned"], 1)
            v.tensor_copy(segt[:], seg_ps[:]).then_inc(q["segt_ready"], 1)
            v.wait_ge(q["seg_back"], 16)
            st(v.tensor_copy(segn[:], segn_i[:]))
            st.wait()
            st(v.tensor_scalar(segn[:, 2, :], segn[:, 2, :], 0.0, None, ALU.is_equal))
            st(v.tensor_tensor(tmp[:], S.node_skip[:], segn[:, 1, :], ALU.subtract))
            st(v.tensor_scalar(last[:], segn[:, 0, :], -1.0, float(EMPTY), ALU.mult, ALU.add))
            st.wait()
            st(v.tensor_tensor(last[:], last[:], segn[:, 2, :], ALU.mult))
            st.wait()
            st(v.tensor_tensor(last[:], last[:], segn[:, 0, :], ALU.add))
            st.wait()
            st(v.tensor_copy(S.end_i[:], last[:]))
            st(v.tensor_tensor(tmp[:], tmp[:], segn[:, 2, :], ALU.mult))
            st.wait()
            st(v.tensor_tensor(tmp[:], tmp[:], segn[:, 1, :], ALU.add))
            st.wait()
            st(v.tensor_copy(S.start_i[:], tmp[:]))
            v.wait_ge(q["heads_in"], 16)
            st(v.tensor_copy(eh_f[:], S.head_i[:]))
            st.wait()
            st(v.tensor_tensor(cond[:], eh_f[:], S.part_end[:], ALU.is_lt))
            st.wait()
            st(v.tensor_tensor(cond[:], cond[:], S.keep[:, 1:2], ALU.mult))
            st(v.tensor_tensor(eh_f[:], eh_f[:], S.edge_dump[:], ALU.subtract))
            st.wait()
            st(v.tensor_tensor(eh_f[:], eh_f[:], cond[:], ALU.mult))
            st.wait()
            st(v.tensor_tensor(eh_f[:], eh_f[:], S.edge_dump[:], ALU.add))
            st.wait()
            st(v.tensor_copy(S.mend_i[:], eh_f[:]))
            st.wait()

        @block.vector
        def _(v):
            st = Steps(v, q["agg_steps"])
            v.sem_inc(q["msg_done"], CREDIT)
            v.sem_inc(q["srcs_done"], CREDIT)
            v.sem_inc(q["onehot_done"], CREDIT)
            v.sem_inc(q["eq_done"], CREDIT)
            v.sem_inc(q["earlier_done"], CREDIT)
            v.sem_inc(q["rows_done"], CREDIT)
            for b in range(2):
                st(v.memset(msg[b][:, :, D + 1:SW], 0.0))
            per_turn = 2 * (GROUPS + 2 * 4 + 3)
            with v.Fori(0, PAIRS) as i:
                st.enter(i, per_turn)
                for b in range(2):
                    c0 = i * (2 * T) + b * T
                    v.wait_ge(q["summed_done"], i * (2 * GROUPS) + (b * GROUPS + 1))
                    v.tensor_scalar(srcs[b][:], S.src_i[:, bass.ds(c0, T)], 0.0, None,
                                    ALU.add).then_inc(q["srcs_done"], 1)
                    v.wait_ge(ef_in[b], i * 32 + 32)
                    v.tensor_tensor(msg[b][:, :, 0:D], ef[b][:], bc(S.exp_w[:, bass.ds(c0, T)], [P, T, D], 2),
                                    ALU.mult).then_inc(q["msg_done"], 1)
                    v.wait_ge(q["srcs_done"], i * 2 + (b + READY))
                    for g in range(GROUPS):
                        at = b * GROUPS + g
                        v.wait_ge(q["row_of_done"], i * (2 * GROUPS) + (at + READY))
                        v.wait_ge(q["summed_done"], i * (2 * GROUPS) + (at + GROUPS))
                        v.tensor_tensor(eq[at % 2][:], row_of[at % 2][:],
                                        bc(srcs[b][:, G * g:G * g + G], [P, G, P], 2),
                                        ALU.is_equal).then_inc(q["eq_done"], 1)
                        if g not in [g0 for g0, g1 in PARTS]:
                            v.wait_ge(q["earlier_done"], i * (2 * GROUPS) + (at - 1 + READY))
                            st(v.tensor_reduce(rank[:, G * (g - 1):G * g], earlier[(at - 1) % 2][:], AX, ALU.add))
                        v.wait_ge(q["eq_done"], i * (2 * GROUPS) + (at + READY))
                        v.tensor_tensor(earlier[at % 2][:], eq[at % 2][:], bc(S.lower[:], [P, G, P], 1),
                                        ALU.mult).then_inc(q["earlier_done"], 1)
                        for part, (g0, g1) in enumerate(PARTS):
                            if g == g1 - 1:
                                v.wait_ge(q["earlier_done"], i * (2 * GROUPS) + (at + READY))
                                st(v.tensor_reduce(rank[:, G * g:G * g1], earlier[at % 2][:], AX, ALU.add))
                                st.wait()
                                now = slice(G * g0, G * g1)
                                st(v.tensor_scalar(rank[:, now], rank[:, now], 1.0, None, ALU.min))
                                st(v.tensor_scalar(target[:, now], srcs[b][:, now], -1.0, S.node_dump[:], ALU.mult, ALU.add))
                                st.wait()
                                st(v.tensor_tensor(target[:, now], target[:, now], rank[:, now], ALU.mult))
                                st.wait()
                                st(v.tensor_tensor(target[:, now], target[:, now], srcs[b][:, now], ALU.add))
                                v.wait_ge(q["scattered"], i * 2 + (b + 1))
                                hold(v)
                                st.wait()
                                v.tensor_copy(rows_i[b][:, now], target[:, now]).then_inc(q["rows_done"], 1)
                    st(v.tensor_scalar(part_i[:, 0, :], S.dst_i[:, bass.ds(c0, T)], P - 1, None, ALU.bitwise_and))
                    st(v.tensor_scalar(part_i[:, 1, :], S.dst_i[:, bass.ds(c0, T)], P.bit_length() - 1, None,
                                       ALU.arith_shift_right))
                    st.wait()
                    st(v.tensor_copy(part16[:], part_i[:]))
                    st.wait()
                    v.wait_ge(q["counted"], i * 2 + (b + FREE))
                    v.tensor_tensor(hi1h[b][:], bc(S.col16[:, 0:KN], [P, T, KN], 1),
                                    bc(part16[:, 1, :], [P, T, KN], 2), ALU.is_equal)
                    v.tensor_tensor(lo1h[b][:], bc(S.col16[:], [P, T, P], 1),
                                    bc(part16[:, 0, :], [P, T, P], 2),
                                    ALU.is_equal).then_inc(q["onehot_done"], 1)
                    v.wait_ge(q["rows_done"], i * 4 + (2 * b + 1 + READY))
                st.leave(PAIRS)
            v.wait_ge(q["loaded"], 16 * n_loads)
            st(v.tensor_copy(dst_f[:], S.dst_i[:]))
            st(v.tensor_copy(prev_f[:], S.prev_i[:]))
            st.wait()
            st(v.tensor_tensor(dst_f[:], dst_f[:], prev_f[:], ALU.not_equal))
            st.wait()
            begin = dst_f[:].rearrange("p (c t) -> p c t", t=T)
            pen = S.pen[:].rearrange("p (c x) -> p c x", x=X)
            keep = S.keep[:].rearrange("p (c x) -> p c x", x=X)
            v.tensor_reduce(S.any_start[:], dst_f[:], AX, ALU.max).then_inc(q["any_done"], 1)
            st(v.tensor_scalar(pen[:, :, 1:X], begin, -BIG, None, ALU.mult))
            st(v.memset(pen[:, :, 0:1], -BIG))
            st(v.tensor_scalar(keep[:, :, 1:X], begin, -1.0, 1.0, ALU.mult, ALU.add))
            st(v.memset(keep[:, :, 0:1], 0.0))
            st.wait()
            segments(v, st)


GK = 4
NODE_GROUPS = [(k, min(GK, KN - k)) for k in range(0, KN, GK)]


def skewed(order):
    for now in range(len(NODE_GROUPS) + max(late for run, late in order)):
        for run, late in order:
            if 0 <= now - late < len(NODE_GROUPS):
                run(now - late)


class Linear:

    def __init__(self, ctx, nc, tag, width):
        self.turned = [ctx.enter_context(nc.psum_tensor(f"{tag}_turned{b}", [D, GK, P], F32)) for b in range(2)]
        self.out = [ctx.enter_context(nc.psum_tensor(f"{tag}_out{b}", [P, GK, width], F32)) for b in range(2)]
        self.col = [ctx.enter_context(nc.sbuf_tensor(f"{tag}_col{b}", [D + 1, GK, P], F32)) for b in range(2)]
        sem = lambda n: nc.alloc_semaphore(f"{tag}_{n}")
        self.turned_done, self.col_done, self.out_done, self.taken = sem("turned"), sem("col"), sem("out"), sem("taken")
        self.ones_done = sem("ones")

    def fill_ones(self, v):
        for col in self.col:
            v.memset(col[D:D + 1], 1.0).then_inc(self.ones_done, 1)

    def turn(self, pe, g, a, a_done, ident):
        k0, n = NODE_GROUPS[g]
        pe.wait_ge(a_done, g + 1)
        if g >= 2:
            pe.wait_ge(self.col_done, g - 1)
        for k in range(n):
            last = pe.transpose(self.turned[g % 2][:, k, :], a[:, k0 + k, :], ident)
        last.then_inc(self.turned_done, 1)

    def copy(self, act, g):
        k0, n = NODE_GROUPS[g]
        act.wait_ge(self.turned_done, g + 1)
        if g >= 2:
            act.wait_ge(self.out_done, g - 1)
        act.activation(self.col[g % 2][0:D, 0:n, :], self.turned[g % 2][:, 0:n, :],
                       ACT.Copy).then_inc(self.col_done, 1)

    def multiply(self, pe, g, weight):
        k0, n = NODE_GROUPS[g]
        pe.wait_ge(self.col_done, g + 1)
        if g == 0:
            pe.wait_ge(self.ones_done, 2)
        if g >= 2:
            pe.wait_ge(self.taken, g - 1)
        for k in range(n):
            last = pe.matmul(self.out[g % 2][:, k, :], self.col[g % 2][0:weight.shape[0], k, :], weight,
                             start=True, stop=True, skip_group_check=True)
        last.then_inc(self.out_done, 1)

    def take(self, act, g, out, func):
        k0, n = NODE_GROUPS[g]
        act.wait_ge(self.out_done, g + 1)
        act.activation(out[:, k0:k0 + n, :], self.out[g % 2][:, 0:n, :], func).then_inc(self.taken, 1)


class Scratch:
    pass


def node_rows(table):
    return table.rearrange("(p k) f -> p k f", k=KN)


class Carry:

    def __init__(self, ctx, nc, S, R, tag, per_feature):
        sb = lambda n, s: ctx.enter_context(nc.sbuf_tensor(f"{tag}_{n}", s, F32))
        ps = lambda n, s: ctx.enter_context(nc.psum_tensor(f"{tag}_{n}", s, F32))
        self.S, self.R, self.per_feature = S, R, per_feature
        self.table = R.state_so if per_feature else R.state
        W = 2 * D if per_feature else SW
        self.ft = sb("ft", [D, 3, P])
        self.carry = sb("carry", [D, 3, P + 1])
        self.ee = sb("ee", [D, 2, P])
        self.row, self.row_m = sb("row", [P, W]), sb("row_m", [P, D])
        self.state = sb("state", [P, 3, D])
        self.mx, self.e2 = sb("mx", [P, D]), sb("e2c", [P, 2, D])
        self.ft_ps, self.in_ps = ps("ft_ps", [D, 3, P]), ps("in_ps", [P, 3, D])
        names = ["final_done", "ft_done", "cy_steps", "ee_ask", "ee_done", "carry_done", "in_done", "rows_in",
                 "e2_ask", "e2_done", "mended", "mend_out"]
        self.q = {n: nc.alloc_semaphore(f"{tag}_{n}") for n in names}

    def pool(self, pool, kept, kept_total):
        q, S = self.q, self.S
        for b in range(2):
            pool.wait_ge(kept[b], kept_total)
        hold(pool)
        at = bass.IndirectOffsetOnAxis(ap=S.head_i[:], axis=0)
        pool.indirect_dma_start(self.row[:], None, self.table, at).then_inc(q["rows_in"], 16)
        if self.per_feature:
            pool.indirect_dma_start(self.row_m[:], None, self.R.state_m, at).then_inc(q["rows_in"], 16)
        pool.wait_ge(q["mended"], 1)
        pool.indirect_dma_start(self.table, bass.IndirectOffsetOnAxis(ap=S.mend_i[:], axis=0), self.row[:], None
                                ).then_inc(q["mend_out"], 16)
        pool.wait_ge(q["mend_out"], 16)

    def tensor(self, pe):
        q, S = self.q, self.S
        pe.wait_ge(q["final_done"], 1)
        for n in range(3):
            last = pe.transpose(self.ft_ps[:, n, :], S.final[:, n, :], S.ident[:])
        last.then_inc(q["ft_done"], 1)
        pe.wait_ge(q["carry_done"], 1)
        for n in range(3):
            last = pe.transpose(self.in_ps[:, n, :], self.carry[:, n, 0:P], S.ident[0:D, 0:D])
        last.then_inc(q["in_done"], 1)

    def scalar(self, act):
        q = self.q
        act.wait_ge(q["ee_ask"], 1)
        act.activation(self.ee[:], self.ee[:], ACT.Exp).then_inc(q["ee_done"], 1)
        act.wait_ge(q["e2_ask"], 1)
        act.activation(self.e2[:], self.e2[:], ACT.Exp).then_inc(q["e2_done"], 1)

    def vector(self, v, finals):
        q, S, per_feature = self.q, self.S, self.per_feature
        ft, carry, ee, row, row_m, state, mx, e2, in_ps = (self.ft, self.carry, self.ee, self.row, self.row_m,
                                                            self.state, self.mx, self.e2, self.in_ps)
        st = Steps(v, q["cy_steps"])
        for n, tile in enumerate(finals):
            st(v.tensor_copy(S.final[:, n, :], tile))
        st.wait()
        v.sem_inc(q["final_done"], 1)
        v.wait_ge(q["ft_done"], 1)
        st(v.tensor_copy(ft[:], self.ft_ps[:]))
        st(v.memset(carry[:, 0, 0:1], -BIG))
        st(v.memset(carry[:, 1:3, 0:1], 0.0))
        st.wait()
        st(v.tensor_tensor_scan(carry[:, 0, 1:P + 1], S.pen_part[:], ft[:, 0, :], -BIG, ALU.add, ALU.max))
        st.wait()
        st(v.tensor_tensor(ee[:, 0, :], carry[:, 0, 0:P], S.pen_part[:], ALU.add))
        st(v.tensor_tensor(ee[:, 1, :], ft[:, 0, :], carry[:, 0, 1:P + 1], ALU.subtract))
        st.wait()
        st(v.tensor_tensor(ee[:, 0, :], ee[:, 0, :], carry[:, 0, 1:P + 1], ALU.subtract))
        st.wait()
        v.sem_inc(q["ee_ask"], 1)
        v.wait_ge(q["ee_done"], 1)
        st(v.tensor_tensor(ft[:, 1:3, :], ft[:, 1:3, :], bc(ee[:, 1, :], [D, 2, P], 1), ALU.mult))
        st.wait()
        st(v.tensor_tensor_scan(carry[:, 1, 1:P + 1], ee[:, 0, :], ft[:, 1, :], 0.0, ALU.mult, ALU.add))
        st(v.tensor_tensor_scan(carry[:, 2, 1:P + 1], ee[:, 0, :], ft[:, 2, :], 0.0, ALU.mult, ALU.add))
        st.wait()
        v.sem_inc(q["carry_done"], 1)
        v.wait_ge(q["rows_in"], 32 if per_feature else 16)
        if per_feature:
            parts = (row_m[:], row[:, 0:D], row[:, D:2 * D])
        else:
            parts = (row[:, D + 1:D + 2].to_broadcast([P, D]), row[:, D:D + 1].to_broadcast([P, D]), row[:, 0:D])
        for n, part in enumerate(parts):
            st(v.tensor_copy(state[:, n, :], part))
        st.wait()
        v.wait_ge(q["in_done"], 1)
        st(v.tensor_tensor(mx[:], state[:, 0, :], in_ps[:, 0, :], ALU.max))
        st.wait()
        st(v.tensor_tensor(e2[:, 0, :], state[:, 0, :], mx[:], ALU.subtract))
        st(v.tensor_tensor(e2[:, 1, :], in_ps[:, 0, :], mx[:], ALU.subtract))
        st.wait()
        v.sem_inc(q["e2_ask"], 1)
        v.wait_ge(q["e2_done"], 1)
        for n in (1, 2):
            st(v.tensor_tensor(state[:, n, :], state[:, n, :], e2[:, 0, :], ALU.mult))
            st(v.tensor_tensor(mx[:] if n == 1 else state[:, 0, :], in_ps[:, n, :], e2[:, 1, :], ALU.mult))
        st.wait()
        if per_feature:
            s_out, s_in, s_add = row[:, 0:D], state[:, 1, :], mx[:]
            o_out = row[:, D:2 * D]
        else:
            s_out, s_in, s_add = row[:, D:D + 1], state[:, 1, 0:1], mx[:, 0:1]
            o_out = row[:, 0:D]
        st(v.tensor_tensor(s_out, s_in, s_add, ALU.add))
        st(v.tensor_tensor(o_out, state[:, 2, :], state[:, 0, :], ALU.add))
        st.wait()
        v.sem_inc(q["mended"], 1)


def index_chunk(io, c):
    return io["src"][:, bass.ds(c * T, T)]


def gather_loop(pool, idx, rows, table, idx_in, landed, used):
    with pool.Fori(0, PAIRS) as i:
        for b in range(2):
            pool.wait_ge(used, i * 2 + (b + FREE))
            hold(pool)
            pool.wait_ge(idx_in[b], i * 16 + 16)
            hold(pool)
            for t in range(T):
                pool.indirect_dma_start(rows[b][:, t, :], None, table,
                                        bass.IndirectOffsetOnAxis(ap=idx[b][:, t:t + 1], axis=0)
                                        ).then_inc(landed[b], 16)


def feature_softmax_phase(nc, io, S, R):
    with nc.cleanup_on_exit(), ExitStack() as ctx:
        sb = lambda n, s: ctx.enter_context(nc.sbuf_tensor(n, s, F32))
        sem = lambda n: nc.alloc_semaphore(n)
        idx = [ctx.enter_context(nc.sbuf_tensor(f"idx{b}", [P, T], I32)) for b in range(2)]
        rows = [sb(f"rows{b}", [P, T, D]) for b in range(2)]
        ef = [sb(f"ef1_{b}", [P, T, D]) for b in range(2)]
        m, pen, mx, dec, wgt, ssum, y, osum = [sb(f"f1_{n}", [P, D, X]) for n in
                                               ("m", "pen", "mx", "dec", "wgt", "ssum", "y", "osum")]
        out_so = [sb(f"out_so{b}", [P, T, 2 * D]) for b in range(2)]
        out_m = [sb(f"out_m{b}", [P, T, D]) for b in range(2)]
        landed = [sem(f"landed{b}") for b in range(2)]
        idx_in = [sem(f"idx_in{b}") for b in range(2)]
        ef_in = [sem(f"ef1_in{b}") for b in range(2)]
        names = ["m_done", "pen_done", "mx_done", "dec_ask", "dec_done", "wgt_ask", "wgt_done",
                 "ssum_done", "y_done", "osum_done", "out_m_done", "out_s_done", "out_o_done", "f1_steps",
                 "f1_init"]
        q = {n: sem(n) for n in names}
        kept = [sem(f"kept{b}") for b in range(2)]
        carry = Carry(ctx, nc, S, R, "c1", True)
        block = ctx.enter_context(nc.Block())
        flat = lambda t: t[:].rearrange("p f x -> p (f x)")

        @block.sync
        def _(sp):
            feats = io["ea64"].rearrange("(p t) f -> p (t f)", p=P)
            so = R.state_so[0:ROWS].rearrange("(p t) w -> p (t w)", p=P)
            sm = R.state_m[0:ROWS].rearrange("(p t) w -> p (t w)", p=P)
            for b in range(2):
                sp.dma_start(idx[b][:], index_chunk(io, b)).then_inc(idx_in[b], 16)
            for b in range(2):
                sp.dma_start(ef[b][:].rearrange("p t f -> p (t f)"), feats[:, b * T * D:(b + 1) * T * D]).then_inc(ef_in[b], 16)
                sp.sem_inc(kept[b], 16)
            with sp.Fori(0, PAIRS - 1) as i:
                for b in range(2):
                    sp.wait_ge(landed[b], i * (T * 16) + T * 16)
                    sp.dma_start(idx[b][:], index_chunk(io, i * 2 + (b + 2))).then_inc(idx_in[b], 16)
                    sp.wait_ge(q["m_done"], i * 2 + (b + READY))
                    sp.dma_start(ef[b][:].rearrange("p t f -> p (t f)"),
                                 feats[:, bass.ds(i * (2 * T * D) + (b + 2) * T * D, T * D)]).then_inc(ef_in[b], 16)
                    sp.wait_ge(q["out_m_done"], i * 2 + (b + READY))
                    hold(sp)
                    sp.dma_start(sm[:, bass.ds(i * (2 * T * D) + b * T * D, T * D)],
                                 out_m[b][:].rearrange("p t f -> p (t f)")).then_inc(kept[b], 16)
                    sp.wait_ge(q["out_s_done"], i * 2 + (b + READY))
                    hold(sp)
                    sp.wait_ge(q["out_o_done"], i * 2 + (b + READY))
                    sp.dma_start(so[:, bass.ds(i * (4 * T * D) + b * 2 * T * D, 2 * T * D)],
                                 out_so[b][:].rearrange("p t f -> p (t f)")).then_inc(kept[b], 16)
            for b in range(2):
                c = 2 * (PAIRS - 1) + b
                sp.wait_ge(q["out_m_done"], c + READY)
                sp.dma_start(sm[:, c * T * D:(c + 1) * T * D],
                             out_m[b][:].rearrange("p t f -> p (t f)")).then_inc(kept[b], 16)
                sp.wait_ge(q["out_s_done"], c + READY)
                sp.wait_ge(q["out_o_done"], c + READY)
                sp.dma_start(so[:, c * 2 * T * D:(c + 1) * 2 * T * D],
                             out_so[b][:].rearrange("p t f -> p (t f)")).then_inc(kept[b], 16)

        @block.gpsimd
        def _(pool):
            gather_loop(pool, idx, rows, R.table, idx_in, landed, q["m_done"])
            carry.pool(pool, kept, 16 + 32 * PAIRS)

        @block.tensor
        def _(pe):
            carry.tensor(pe)

        @block.scalar
        def _(act):
            for n in ("pen_done", "dec_done", "wgt_done", "out_m_done", "out_s_done", "out_o_done"):
                act.sem_inc(q[n], CREDIT)
            act.wait_ge(q["f1_init"], 1)
            with act.Fori(0, PAIRS) as i:
                for b in range(2):
                    c = lambda k: i * 2 + (b + k)
                    act.wait_ge(q["dec_ask"], c(PREV))
                    hold(act)
                    act.activation(pen[:], bc(S.pen[:, bass.ds(i * (2 * X) + b * X, X)], [P, D, X], 1),
                                   ACT.Copy).then_inc(q["pen_done"], 1)
                    act.wait_ge(q["mx_done"], c(READY))
                    act.wait_ge(kept[b], i * 32 + 16)
                    act.activation(turned(out_m[b][:]), mx[:, :, 1:X], ACT.Copy).then_inc(q["out_m_done"], 1)
                    act.wait_ge(q["dec_ask"], c(READY))
                    act.activation(dec[:, :, 1:X], dec[:, :, 1:X], ACT.Exp).then_inc(q["dec_done"], 1)
                    act.wait_ge(q["wgt_ask"], c(READY))
                    act.activation(wgt[:, :, 1:X], wgt[:, :, 1:X], ACT.Exp).then_inc(q["wgt_done"], 1)
                    act.wait_ge(q["ssum_done"], c(READY))
                    act.activation(turned(out_so[b][:, :, 0:D]), ssum[:, :, 1:X], ACT.Copy).then_inc(q["out_s_done"], 1)
                    act.wait_ge(q["osum_done"], c(READY))
                    act.activation(turned(out_so[b][:, :, D:2 * D]), osum[:, :, 1:X], ACT.Copy).then_inc(q["out_o_done"], 1)
                    act.wait_ge(q["out_m_done"], c(READY))
                    act.wait_ge(q["out_s_done"], c(READY))
                    hold(act)
            carry.scalar(act)

        @block.vector
        def _(v):
            st = Steps(v, q["f1_steps"])
            for n in ("m_done", "mx_done", "dec_ask", "wgt_ask", "ssum_done", "y_done", "osum_done"):
                v.sem_inc(q[n], CREDIT)
            st(v.memset(mx[:], -BIG))
            st(v.memset(ssum[:], 0.0))
            st(v.memset(osum[:], 0.0))
            st(v.memset(dec[:], 0.0))
            st.wait()
            v.sem_inc(q["f1_init"], 1)
            with v.Fori(0, PAIRS) as i:
                st.enter(i, 2 * 4)
                for b in range(2):
                    c = lambda k: i * 2 + (b + k)
                    v.wait_ge(landed[b], i * (T * 16) + T * 16)
                    hold(v)
                    v.wait_ge(ef_in[b], i * 16 + 16)
                    v.tensor_tensor(turned(m[:, :, 1:X]), rows[b][:], ef[b][:], ALU.add).then_inc(q["m_done"], 1)
                    st(v.tensor_copy(m[:, :, 0:1], mx[:, :, T:X]))
                    v.wait_ge(q["m_done"], c(READY))
                    hold(v)
                    v.wait_ge(q["out_m_done"], c(PREV))
                    hold(v)
                    v.wait_ge(q["pen_done"], c(READY))
                    hold(v)
                    st.wait()
                    v.tensor_tensor_scan(flat(mx), flat(pen), flat(m), 0.0, ALU.add, ALU.max).then_inc(q["mx_done"], 1)
                    v.wait_ge(q["mx_done"], c(READY))
                    hold(v)
                    v.wait_ge(q["osum_done"], c(PREV))
                    st(v.tensor_tensor(dec[:, :, 1:X], mx[:, :, 0:T], pen[:, :, 1:X], ALU.add))
                    st.wait()
                    v.tensor_tensor(dec[:, :, 1:X], dec[:, :, 1:X], mx[:, :, 1:X], ALU.subtract).then_inc(q["dec_ask"], 1)
                    v.tensor_tensor(wgt[:, :, 1:X], m[:, :, 1:X], mx[:, :, 1:X], ALU.subtract).then_inc(q["wgt_ask"], 1)
                    st(v.tensor_copy(wgt[:, :, 0:1], ssum[:, :, T:X]))
                    v.wait_ge(q["dec_done"], c(READY))
                    hold(v)
                    v.wait_ge(q["out_s_done"], c(PREV))
                    hold(v)
                    v.wait_ge(q["wgt_done"], c(READY))
                    hold(v)
                    st.wait()
                    v.tensor_tensor_scan(flat(ssum), flat(dec), flat(wgt), 0.0, ALU.mult, ALU.add).then_inc(q["ssum_done"], 1)
                    v.tensor_tensor(y[:, :, 1:X], m[:, :, 1:X], wgt[:, :, 1:X], ALU.mult).then_inc(q["y_done"], 1)
                    st(v.tensor_copy(y[:, :, 0:1], osum[:, :, T:X]))
                    v.wait_ge(q["y_done"], c(READY))
                    hold(v)
                    v.wait_ge(q["out_o_done"], c(PREV))
                    hold(v)
                    st.wait()
                    v.tensor_tensor_scan(flat(osum), flat(dec), flat(y), 0.0, ALU.mult, ALU.add).then_inc(q["osum_done"], 1)
                    v.wait_ge(q["osum_done"], c(READY))
                    hold(v)
                    v.wait_ge(q["ssum_done"], c(READY))
                    hold(v)
                st.leave(PAIRS)
            carry.vector(v, (mx[:, :, T], ssum[:, :, T], osum[:, :, T]))


def scalar_softmax_phase(nc, io, S, R, layer):
    gat = layer == LAYERS
    tag = f"e{layer}"
    GW = SW if gat else D
    with nc.cleanup_on_exit(), ExitStack() as ctx:
        sb = lambda n, s: ctx.enter_context(nc.sbuf_tensor(f"{tag}_{n}", s, F32))
        sem = lambda n: nc.alloc_semaphore(f"{tag}_{n}")
        idx = [ctx.enter_context(nc.sbuf_tensor(f"{tag}_idx{b}", [P, T], I32)) for b in range(2)]
        rows = [sb(f"rows{b}", [P, T, GW]) for b in range(2)]
        FW = DE if gat else D
        side = [sb(f"side{b}", [P, T, FW]) for b in range(2)]
        if gat:
            inj1, keep1, dst_score = sb("inj1", [P, TILES]), sb("keep1", [P, TILES]), sb("dst_score", [P, TILES])
            z = sb("z", [P, T, DE])
        else:
            kx, inj, xr = sb("kx", [P, D, X]), sb("inj", [P, D, X]), sb("xr", [P, D, X])
            z = sb("z", [P, T, D])
        score, mrow, srow, e2 = sb("score", [P, X]), sb("mrow", [P, X]), sb("srow", [P, X]), sb("e2", [P, 2, X])
        dx, y, osum = sb("dx", [P, D, X]), sb("y", [P, D, X]), sb("osum", [P, D, X])
        out = [sb(f"out{b}", [P, T, SW]) for b in range(2)]
        landed = [sem(f"landed{b}") for b in range(2)]
        idx_in = [sem(f"idx_in{b}") for b in range(2)]
        side_in = [sem(f"side_in{b}") for b in range(2)]
        kept = [sem(f"kept{b}") for b in range(2)]
        carry = Carry(ctx, nc, S, R, f"c{layer + 2}", False)
        names = ["kx_done", "inj_done", "xr_done", "z_done", "exp_ask", "exp_done", "dx_done", "y_done",
                 "srow_done", "osum_done", "out_sm_done", "out_o_done", "steps", "init", "inj1_in", "fdot_done"]
        q = {n: sem(n) for n in names}
        block = ctx.enter_context(nc.Block())
        flat = lambda t: t[:].rearrange("p f x -> p (f x)")
        side_used = q["fdot_done"] if gat else q["inj_done"]

        @block.sync
        def _(sp):
            src = io["ea16"] if gat else R.inject[0:ROWS]
            feats = src.rearrange("(p t) f -> p (t f)", p=P)
            states = R.state[0:ROWS].rearrange("(p t) w -> p (t w)", p=P)
            W = T * FW
            if gat:
                sp.dma_start(inj1[:], R.inject1[0:ROWS].rearrange("(p t) f -> p (t f)", p=P)).then_inc(q["inj1_in"], 16)
            for b in range(2):
                sp.dma_start(idx[b][:], index_chunk(io, b)).then_inc(idx_in[b], 16)
            for b in range(2):
                sp.dma_start(side[b][:].rearrange("p t f -> p (t f)"), feats[:, b * W:(b + 1) * W]).then_inc(side_in[b], 16)
                sp.sem_inc(kept[b], 16)
            with sp.Fori(0, PAIRS - 1) as i:
                for b in range(2):
                    sp.wait_ge(landed[b], i * (T * 16) + T * 16)
                    sp.dma_start(idx[b][:], index_chunk(io, i * 2 + (b + 2))).then_inc(idx_in[b], 16)
                    sp.wait_ge(side_used, i * 2 + (b + READY))
                    sp.dma_start(side[b][:].rearrange("p t f -> p (t f)"),
                                 feats[:, bass.ds(i * (2 * W) + (b + 2) * W, W)]).then_inc(side_in[b], 16)
                    sp.wait_ge(q["out_sm_done"], i * 2 + (b + READY))
                    hold(sp)
                    sp.wait_ge(q["out_o_done"], i * 2 + (b + READY))
                    sp.dma_start(states[:, bass.ds(i * (2 * T * SW) + b * T * SW, T * SW)],
                                 out[b][:].rearrange("p t f -> p (t f)")).then_inc(kept[b], 16)
            for b in range(2):
                c = 2 * (PAIRS - 1) + b
                sp.wait_ge(q["out_sm_done"], c + READY)
                sp.wait_ge(q["out_o_done"], c + READY)
                sp.dma_start(states[:, c * T * SW:(c + 1) * T * SW],
                             out[b][:].rearrange("p t f -> p (t f)")).then_inc(kept[b], 16)

        @block.gpsimd
        def _(pool):
            table = R.table3 if gat else R.table
            gather_loop(pool, idx, rows, table, idx_in, landed, q["y_done"])
            carry.pool(pool, kept, 16 + 16 * PAIRS)

        @block.tensor
        def _(pe):
            carry.tensor(pe)

        @block.scalar
        def _(act):
            for n in ("kx_done", "inj_done", "exp_done", "dx_done", "out_o_done"):
                act.sem_inc(q[n], CREDIT)
            act.wait_ge(q["init"], 1)
            with act.Fori(0, PAIRS) as i:
                for b in range(2):
                    c = lambda k: i * 2 + (b + k)
                    if not gat:
                        act.wait_ge(q["xr_done"], c(PREV))
                        hold(act)
                        act.activation(kx[:], bc(S.keep[:, bass.ds(i * (2 * X) + b * X, X)], [P, D, X], 1),
                                       ACT.Copy).then_inc(q["kx_done"], 1)
                        act.wait_ge(side_in[b], i * 16 + 16)
                        act.activation(inj[:, :, 1:X], turned(side[b][:]), ACT.Copy).then_inc(q["inj_done"], 1)
                    act.wait_ge(q["exp_ask"], c(READY))
                    act.activation(e2[:, :, 1:X], e2[:, :, 1:X], ACT.Exp).then_inc(q["exp_done"], 1)
                    act.wait_ge(q["osum_done"], c(PREV))
                    hold(act)
                    act.wait_ge(q["exp_done"], c(READY))
                    act.activation(dx[:], bc(e2[:, 0, :], [P, D, X], 1), ACT.Copy).then_inc(q["dx_done"], 1)
                    act.wait_ge(kept[b], i * 16 + 16)
                    hold(act)
                    act.wait_ge(q["osum_done"], c(READY))
                    act.activation(turned(out[b][:, :, 0:D]), osum[:, :, 1:X], ACT.Copy).then_inc(q["out_o_done"], 1)
            carry.scalar(act)

        @block.vector
        def _(v):
            st = Steps(v, q["steps"])
            for n in ("xr_done", "z_done", "exp_ask", "y_done", "srow_done", "osum_done", "out_sm_done", "fdot_done"):
                v.sem_inc(q[n], CREDIT)
            st(v.memset(mrow[:], -BIG))
            st(v.memset(srow[:], 0.0))
            st(v.memset(osum[:], 0.0))
            st(v.memset(e2[:], 0.0))
            if gat:
                st(v.tensor_copy(keep1[:].rearrange("p (c t) -> p c t", t=T),
                                 S.keep[:].rearrange("p (c x) -> p c x", x=X)[:, :, 1:X]))
                v.wait_ge(q["inj1_in"], 16)
                st.wait()
                st(v.tensor_tensor_scan(dst_score[:], keep1[:], inj1[:], S.head_row[:, D + 1:D + 2], ALU.mult, ALU.add))
            else:
                st(v.tensor_copy(xr[:, :, T], S.head_row[:, 0:D]))
            st.wait()
            v.sem_inc(q["init"], 1)
            per_chunk = 11
            with v.Fori(0, PAIRS) as i:
                st.enter(i, 2 * per_chunk)
                for b in range(2):
                    c = lambda k: i * 2 + (b + k)
                    pen = S.pen[:, bass.ds(i * (2 * X) + b * X, X)]
                    if gat:
                        v.wait_ge(side_in[b], i * 16 + 16)
                        v.tensor_tensor(z[:], side[b][:], bc(S.wa[:, D:D + DE], [P, T, DE], 1),
                                        ALU.mult).then_inc(q["fdot_done"], 1)
                        v.wait_ge(q["fdot_done"], c(READY))
                        hold(v)
                        st(v.tensor_reduce(score[:, 1:X], z[:], AX, ALU.add))
                        v.wait_ge(landed[b], i * (T * 16) + T * 16)
                        hold(v)
                        st.wait()
                        st(v.tensor_tensor(score[:, 1:X], score[:, 1:X], rows[b][:, :, D], ALU.add))
                        st.wait()
                        st(v.tensor_tensor(score[:, 1:X], score[:, 1:X], dst_score[:, bass.ds(i * (2 * T) + b * T, T)], ALU.add))
                        st.wait()
                        st(v.scalar_tensor_tensor(score[:, 1:X], score[:, 1:X], SLOPE, score[:, 1:X], ALU.mult, ALU.max))
                    else:
                        v.wait_ge(q["kx_done"], c(READY))
                        hold(v)
                        v.wait_ge(q["inj_done"], c(READY))
                        hold(v)
                        st(v.tensor_copy(inj[:, :, 0], xr[:, :, T]))
                        st.wait()
                        v.tensor_tensor_scan(flat(xr), flat(kx), flat(inj), 0.0, ALU.mult, ALU.add).then_inc(q["xr_done"], 1)
                        v.wait_ge(landed[b], i * (T * 16) + T * 16)
                        hold(v)
                        v.wait_ge(q["xr_done"], c(READY))
                        st(v.tensor_tensor(z[:], rows[b][:], turned(xr[:, :, 1:X]), ALU.add))
                        st.wait()
                        st(v.scalar_tensor_tensor(z[:], z[:], SLOPE, z[:], ALU.mult, ALU.max))
                        st.wait()
                        v.tensor_tensor(z[:], z[:], bc(S.att[:, layer * D:(layer + 1) * D], [P, T, D], 1),
                                        ALU.mult).then_inc(q["z_done"], 1)
                        v.wait_ge(q["z_done"], c(READY))
                        st(v.tensor_reduce(score[:, 1:X], z[:], AX, ALU.add))
                    st(v.tensor_copy(score[:, 0:1], mrow[:, T:X]))
                    st.wait()
                    st(v.tensor_tensor_scan(mrow[:], pen, score[:], 0.0, ALU.add, ALU.max))
                    st.wait()
                    st(v.tensor_tensor(e2[:, 0, 1:X], mrow[:, 0:T], pen[:, 1:X], ALU.add))
                    st(v.tensor_copy(e2[:, 1, 0:1], srow[:, T:X]))
                    st.wait()
                    st(v.tensor_tensor(e2[:, 1, 1:X], score[:, 1:X], mrow[:, 1:X], ALU.subtract))
                    st.wait()
                    v.tensor_tensor(e2[:, 0, 1:X], e2[:, 0, 1:X], mrow[:, 1:X], ALU.subtract).then_inc(q["exp_ask"], 1)
                    v.wait_ge(q["exp_ask"], c(READY))
                    hold(v)
                    v.wait_ge(q["exp_done"], c(READY))
                    hold(v)
                    v.tensor_tensor(turned(y[:, :, 1:X]), rows[b][:, :, 0:D], bc(e2[:, 1, 1:X], [P, T, D], 2),
                                    ALU.mult).then_inc(q["y_done"], 1)
                    st(v.tensor_copy(y[:, :, 0], osum[:, :, T]))
                    v.tensor_tensor_scan(srow[:], e2[:, 0, :], e2[:, 1, :], 0.0, ALU.mult, ALU.add).then_inc(q["srow_done"], 1)
                    v.wait_ge(q["srow_done"], c(READY))
                    hold(v)
                    v.wait_ge(kept[b], i * 16 + 16)
                    st(v.tensor_copy(out[b][:, :, D], srow[:, 1:X]))
                    v.tensor_copy(out[b][:, :, D + 1], mrow[:, 1:X]).then_inc(q["out_sm_done"], 1)
                    v.wait_ge(q["dx_done"], c(READY))
                    hold(v)
                    v.wait_ge(q["out_o_done"], c(PREV))
                    hold(v)
                    v.wait_ge(q["y_done"], c(READY))
                    hold(v)
                    v.wait_ge(q["out_sm_done"], c(READY))
                    hold(v)
                    st.wait()
                    v.tensor_tensor_scan(flat(osum), flat(dx), flat(y), 0.0, ALU.mult, ALU.add).then_inc(q["osum_done"], 1)
                    v.wait_ge(q["osum_done"], c(READY))
                    hold(v)
                st.leave(PAIRS)
            carry.vector(v, (mrow[:, T:X].to_broadcast([P, D]), srow[:, T:X].to_broadcast([P, D]), osum[:, :, T]))


def nodes_phase(nc, io, S, R, stage):
    tag = f"n{stage}"
    layer = stage - 2
    mid, norm, edge_rows = stage in (2, 3), stage in (0, 1, 4), 1 <= stage <= 3
    W = 2 * D if stage == 1 else SW
    with nc.cleanup_on_exit(), ExitStack() as ctx:
        sb = lambda n, s: ctx.enter_context(nc.sbuf_tensor(f"{tag}_{n}", s, F32))
        sem = lambda n: nc.alloc_semaphore(f"{tag}_{n}")
        node_state = sb("state", [P, KN, W]) if stage else None
        part = None if stage else [sb(f"part{k}", [P, KN, SW]) for k in range(TABLES)]
        new, sq = sb("new", [P, KN, D]), sb("sq", [P, KN, D])
        stat, root = sb("stat", [P, KN]), sb("root", [P, KN])
        rec = sb("rec", [P, KN, D]) if stage == 1 else sb("rec", [P, KN])
        first = Linear(ctx, nc, tag + "a", D) if stage == 1 else None
        ahead = Linear(ctx, nc, tag + "b", 2 * D if edge_rows else D) if 1 <= stage <= 4 else None
        lr = sb("lr", [P, KN, 2 * D]) if edge_rows else None
        t3 = sb("t3", [P, KN, SW]) if stage == 4 else None
        q = {n: sem(n) for n in ("steps", "new_done", "gelu_done", "centred", "sq_done", "var_done", "root_done",
                                 "scaled", "relu_done", "t3_done", "stored", "inject", "head",
                                 "half_done", "kept", "rec_done")}
        nodes_in = [sem(f"nodes_in{g}") for g in range(len(NODE_GROUPS))]
        block = ctx.enter_context(nc.Block())
        state_table = R.state_so if stage == 1 else R.state
        row_done = ahead.taken if edge_rows else q["relu_done"] if stage == 0 else q["t3_done"]
        cut = lambda t, g: t[:, NODE_GROUPS[g][0]:sum(NODE_GROUPS[g])]

        @block.sync
        def _(sp):
            if stage == 0:
                for g in range(len(NODE_GROUPS)):
                    for k in range(TABLES):
                        sp.dma_start(cut(part[k], g), cut(node_rows(R.acc[k][0:NODES]), g)).then_inc(nodes_in[g], 16)
            for g in range(len(NODE_GROUPS)):
                if stage == 0:
                    sp.wait_ge(row_done, g + 1)
                    sp.dma_start(cut(node_rows(R.table), g), cut(S.h, g)).then_inc(q["stored"], 16)
                elif edge_rows:
                    sp.wait_ge(row_done, g + 1)
                    sp.dma_start(cut(node_rows(R.table), g), cut(lr, g)[:, :, 0:D]).then_inc(q["stored"], 16)
                    sp.dma_start(cut(node_rows(R.table_r), g), cut(lr, g)[:, :, D:2 * D]).then_inc(q["stored"], 16)
                elif stage == 4:
                    sp.wait_ge(row_done, g + 1)
                    sp.dma_start(cut(node_rows(R.table3), g), cut(t3, g)).then_inc(q["stored"], 16)
                else:
                    sp.wait_ge(q["new_done"], g + 1)
                    sp.dma_start(cut(io["out"].rearrange("p (k f) -> p k f", f=D), g), cut(new, g)).then_inc(q["stored"], 16)
            sp.wait_ge(q["stored"], 16 * len(NODE_GROUPS) * (2 if edge_rows else 1))

        @block.gpsimd
        def _(pool):
            if stage == 0:
                def half(g):
                    pool.wait_ge(nodes_in[g], 16 * TABLES)
                    for k in (0, 2):
                        pool.tensor_tensor(cut(part[k], g), cut(part[k], g), cut(part[k + 1], g),
                                           ALU.add).then_inc(q["half_done"], 1)

                def keep(g):
                    pool.wait_ge(q["relu_done"], g + 1)
                    pool.tensor_tensor(cut(S.xres, g), cut(S.xres, g), cut(S.h, g),
                                       ALU.add).then_inc(q["kept"], 1)

                skewed([(half, 0), (keep, 5)])
                pool.wait_ge(q["kept"], len(NODE_GROUPS))
                return
            for g, (k0, n) in enumerate(NODE_GROUPS):
                for k in range(k0, k0 + n):
                    pool.indirect_dma_start(node_state[:, k, :], None, state_table,
                                            bass.IndirectOffsetOnAxis(ap=S.end_i[:, k:k + 1], axis=0)
                                            ).then_inc(nodes_in[g], 16)
            if stage == 5:
                for g, (k0, n) in enumerate(NODE_GROUPS):
                    pool.wait_ge(nodes_in[g], 16 * n)
                return
            for g, (k0, n) in enumerate(NODE_GROUPS):
                pool.wait_ge(row_done, g + 1)
                for k in range(k0, k0 + n):
                    at = bass.IndirectOffsetOnAxis(ap=S.start_i[:, k:k + 1], axis=0)
                    if edge_rows:
                        pool.indirect_dma_start(R.inject, at, lr[:, k, D:2 * D], None).then_inc(q["inject"], 16)
                    else:
                        pool.indirect_dma_start(R.inject1, at, t3[:, k, D + 1:D + 2], None).then_inc(q["inject"], 16)
            pool.wait_ge(q["stored"], 16 * len(NODE_GROUPS) * (2 if edge_rows else 1))
            at = bass.IndirectOffsetOnAxis(ap=S.dst0[:], axis=0)
            if edge_rows:
                pool.indirect_dma_start(S.head_row[:, 0:D], None, R.table_r, at).then_inc(q["head"], 16)
            else:
                pool.indirect_dma_start(S.head_row[:], None, R.table3, at).then_inc(q["head"], 16)
            pool.wait_ge(q["inject"], 16 * KN)
            pool.wait_ge(q["head"], 16)

        @block.tensor
        def _(pe):
            ident = S.ident[:]
            w_ahead = S.wlr[:, layer + 1, :] if edge_rows else S.w3[:]
            turn1 = lambda g: first.turn(pe, g, new, q["new_done"], ident)
            mul1 = lambda g: first.multiply(pe, g, S.w1[:])
            turn2 = lambda g: ahead.turn(pe, g, S.h if norm else new, q["relu_done"] if norm else q["gelu_done"], ident)
            mul2 = lambda g: ahead.multiply(pe, g, w_ahead)
            if stage == 1:
                skewed([(turn1, 0), (turn2, 8), (mul1, 1), (mul2, 9)])
            elif stage == 4:
                skewed([(turn2, 5), (mul2, 6)])
            elif mid:
                skewed([(turn2, 0), (mul2, 0)])

        @block.scalar
        def _(act):
            def gelu(g):
                act.wait_ge(q["new_done"], g + 1)
                act.activation(cut(new, g), cut(new, g), ACT.Gelu).then_inc(q["gelu_done"], 1)

            def square(g):
                act.wait_ge(q["centred"], g + 1)
                act.activation(cut(sq, g), cut(S.h, g), ACT.Square).then_inc(q["sq_done"], 1)

            def sqrt(g):
                act.wait_ge(q["var_done"], g + 1)
                act.activation(cut(root, g), cut(stat, g), ACT.Sqrt).then_inc(q["root_done"], 1)

            def relu(g):
                act.wait_ge(q["scaled"], g + 1)
                if stage == 0:
                    k0, n = NODE_GROUPS[g]
                    for k in range(k0, k0 + n):
                        last = act.activation(S.h[:, k, :], S.h[:, k, :], ACT.Relu, scale=root[:, k:k + 1])
                    last.then_inc(q["relu_done"], 1)
                else:
                    act.activation(cut(S.h, g), cut(S.h, g), ACT.Relu).then_inc(q["relu_done"], 1)

            def weighted(g):
                k0, n = NODE_GROUPS[g]
                act.wait_ge(q["rec_done"], g + 1)
                for k in range(k0, k0 + n):
                    last = act.activation(new[:, k, :], part[0][:, k, 0:D], ACT.Copy, scale=rec[:, k:k + 1])
                last.then_inc(q["new_done"], 1)

            copy1, take1 = (lambda g: first.copy(act, g)), (lambda g: first.take(act, g, new, ACT.Relu))
            copy2 = lambda g: ahead.copy(act, g)
            take2 = lambda g: ahead.take(act, g, lr if edge_rows else t3[:, :, 0:D], ACT.Copy)
            if stage == 0:
                skewed([(relu, 4), (sqrt, 3), (square, 2), (weighted, 1)])
            elif stage == 1:
                skewed([(take1, 2), (copy1, 0), (square, 4), (sqrt, 5), (relu, 7), (take2, 10), (copy2, 8)])
            elif stage == 4:
                skewed([(relu, 4), (take2, 6), (copy2, 5), (sqrt, 3), (gelu, 0), (square, 2)])
            elif mid:
                skewed([(gelu, 0), (copy2, 0), (take2, 0)])

        @block.vector
        def _(v):
            st = Steps(v, q["steps"])
            for linear in (first, ahead):
                if linear:
                    linear.fill_ones(v)

            def output(g):
                k0, n = NODE_GROUPS[g]
                state, shape = cut(node_state, g) if stage else None, [P, n, D]
                if stage == 0:
                    v.wait_ge(nodes_in[g], 16 * TABLES)
                    v.wait_ge(q["half_done"], 2 * g + 2)
                    st(v.tensor_tensor(cut(part[0], g), cut(part[0], g), cut(part[2], g), ALU.add))
                    st.wait()
                    st(v.tensor_scalar(cut(rec, g), cut(part[0], g)[:, :, D], 1.2e-38, None, ALU.max))
                    st.wait()
                    v.reciprocal(cut(rec, g), cut(rec, g)).then_inc(q["rec_done"], 1)
                    return
                v.wait_ge(nodes_in[g], 16 * n)
                if stage == 1:
                    st(v.tensor_scalar(cut(rec, g), state[:, :, 0:D], 1.2e-38, None, ALU.max))
                    st.wait()
                    st(v.reciprocal(cut(rec, g), cut(rec, g)))
                    st.wait()
                    v.tensor_tensor(cut(new, g), state[:, :, D:2 * D], cut(rec, g), ALU.mult).then_inc(q["new_done"], 1)
                    return
                if stage == 5:
                    st(v.tensor_scalar(cut(rec, g), state[:, :, D], 1e-16, None, ALU.add))
                    st.wait()
                    st(v.reciprocal(cut(rec, g), cut(rec, g)))
                else:
                    st(v.reciprocal(cut(rec, g), state[:, :, D]))
                st.wait()
                st(v.tensor_tensor(cut(new, g), state[:, :, 0:D], bc(cut(rec, g), shape, 2), ALU.mult))
                st.wait()
                bias = S.bias3[:] if stage == 5 else S.bias2[:, layer * D:(layer + 1) * D]
                if stage == 5:
                    st(v.tensor_tensor(cut(new, g), cut(new, g), bc(bias, shape, 1), ALU.add))
                    st.wait()
                    v.tensor_tensor(cut(new, g), cut(new, g), cut(S.xres, g), ALU.add).then_inc(q["new_done"], 1)
                else:
                    v.tensor_tensor(cut(new, g), cut(new, g), bc(bias, shape, 1), ALU.add).then_inc(q["new_done"], 1)

            def centre(g):
                k0, n = NODE_GROUPS[g]
                v.wait_ge((q["new_done"], first and first.taken, 0, 0, q["gelu_done"])[stage], g + 1)
                st(v.tensor_tensor(cut(S.xres, g), cut(S.xres, g), cut(new, g), ALU.add))
                st.wait()
                st(v.tensor_reduce(cut(stat, g), cut(S.xres, g), AX, ALU.add))
                st.wait()
                st(v.tensor_scalar(cut(stat, g), cut(stat, g), -1.0 / D, None, ALU.mult))
                st.wait()
                v.tensor_tensor(cut(S.h, g), cut(S.xres, g), bc(cut(stat, g), [P, n, D], 2),
                                ALU.add).then_inc(q["centred"], 1)

            def variance(g):
                v.wait_ge(q["sq_done"], g + 1)
                v.wait_ge(q["centred"], g + 1)
                st(v.tensor_reduce(cut(stat, g), cut(sq, g), AX, ALU.add))
                st.wait()
                v.tensor_scalar(cut(stat, g), cut(stat, g), 1.0 / D, EPS, ALU.mult, ALU.add).then_inc(q["var_done"], 1)

            def scale(g):
                k0, n = NODE_GROUPS[g]
                v.wait_ge(q["root_done"], g + 1)
                if stage == 0:
                    v.reciprocal(cut(root, g), cut(root, g)).then_inc(q["scaled"], 1)
                    return
                st(v.reciprocal(cut(root, g), cut(root, g)))
                st.wait()
                v.tensor_tensor(cut(S.h, g), cut(S.h, g), bc(cut(root, g), [P, n, D], 2), ALU.mult).then_inc(q["scaled"], 1)

            def scores(g):
                k0, n = NODE_GROUPS[g]
                v.wait_ge(ahead.taken, g + 1)
                for col, at in ((D, D + DE), (D + 1, 0)):
                    st(v.tensor_tensor(cut(sq, g), cut(t3, g)[:, :, 0:D], bc(S.wa[:, at:at + D], [P, n, D], 1), ALU.mult))
                    st.wait()
                    last = v.tensor_reduce(cut(t3, g)[:, :, col], cut(sq, g), AX, ALU.add)
                    if col == D:
                        st(last)
                        st.wait()
                last.then_inc(q["t3_done"], 1)

            if stage == 0:
                skewed([(scale, 4), (variance, 3), (output, 0), (centre, 2)])
            elif stage == 1:
                skewed([(output, 0), (centre, 3), (variance, 5), (scale, 6)])
            elif stage == 4:
                skewed([(scale, 4), (output, 0), (variance, 3), (centre, 2), (scores, 7)])
            else:
                skewed([(output, 0)])


def build_program(nc, io):
    with ExitStack() as ctx:
        S, R = Scratch(), Scratch()
        sb = lambda n, s, d=F32: ctx.enter_context(nc.sbuf_tensor(n, s, d))
        dram = lambda n, s, d=F32: nc.dram_tensor(n, s, d, kind="Internal").ap()
        S.pen = sb("pen", [P, CHUNKS * X])
        S.keep = sb("keep", [P, CHUNKS * X])
        S.xres = sb("xres", [P, KN, D])
        S.h = sb("h", [P, KN, D])
        S.ident, S.upto, S.ones = sb("ident", [P, P]), sb("upto", [P, P]), sb("ones", [P, P])
        S.w1, S.w3, S.wlr = sb("w1", [D + 1, D]), sb("w3", [D, D]), sb("wlr", [D + 1, LAYERS, 2 * D])
        S.bias3, S.wa = sb("bias3", [P, D]), sb("wa", [P, 2 * D + DE])
        S.att, S.bias2 = sb("att", [P, LAYERS * D]), sb("bias2", [P, LAYERS * D])
        S.pf, S.node_dump, S.edge_dump = sb("pf", [P, 1]), sb("node_dump", [P, 1]), sb("edge_dump", [P, 1])
        S.part_end, S.any_start = sb("part_end", [P, 1]), sb("any_start", [P, 1])
        S.node_skip = sb("node_skip", [P, KN])
        S.count = sb("count", [P, KN])
        S.end_i, S.start_i = sb("end_i", [P, KN], I32), sb("start_i", [P, KN], I32)
        S.dst0, S.head_i, S.mend_i = sb("dst0", [P, 1], I32), sb("head_i", [P, 1], I32), sb("mend_i", [P, 1], I32)
        S.pen_part = sb("pen_part", [D, P])
        S.head_row = sb("head_row", [P, SW])
        S.final = sb("final", [P, 3, D])
        R.acc = [dram(f"acc{k}", (ACC_ROWS, SW)) for k in range(TABLES)]
        R.inject, R.inject1 = dram("inject", (ROWS + NODES, D)), dram("inject1", (ROWS + NODES, 1))
        R.seg_info, R.last_edge = dram("seg_info", (3, NODES), I32), dram("last_edge", (NODES, 1), I32)
        R.table, R.table_r, R.table3 = dram("table", (NODES, D)), dram("table_r", (NODES, D)), dram("table3", (NODES, SW))
        R.state_so, R.state_m, R.state = dram("state_so", (EMPTY + 1, 2 * D)), dram("state_m", (ROWS, D)), dram("state", (EMPTY + 1, SW))

        with ExitStack() as early:
            sbe = lambda n, s, d=F32: early.enter_context(nc.sbuf_tensor(n, s, d))
            S.src_i, S.dst_i = sbe("src_i", [P, TILES], I32), sbe("dst_i", [P, TILES], I32)
            S.exp_w = sbe("exp_w", [P, TILES])
            S.prev_i = sbe("prev_i", [P, TILES], I32)
            S.lower, S.col16 = sbe("lower", [P, P]), sbe("col16", [P, P], BF16)
            S.zeros = sbe("zeros", [P, ACC_ROWS // P * SW])
            setup_phase(nc, io, S)
            aggregate_phase(nc, io, S, R)
        nodes_phase(nc, io, S, R, 0)
        feature_softmax_phase(nc, io, S, R)
        nodes_phase(nc, io, S, R, 1)
        for layer in range(LAYERS + 1):
            scalar_softmax_phase(nc, io, S, R, layer)
            nodes_phase(nc, io, S, R, layer + 2)


def laid_out(x, src, dst, edge_attr_16, edge_attr_64, edge_weight1, L1_gnn_W, L1_gnn_b, L2_gnn_Wl, L2_gnn_bl,
             L2_gnn_Wr, L2_gnn_br, L2_gnn_att, L2_gnn_bias, L3_gnn_W, L3_gnn_w_att, L3_gnn_bias):
    import numpy as np

    def rows(a, n, fill=0):
        a = np.asarray(a)
        return np.concatenate([a, np.full((n - a.shape[0],) + a.shape[1:], fill, a.dtype)])

    out = {
        "x": rows(x, NODES).reshape(P, KN * D),
        "src": rows(src, ROWS, NODES - 1).reshape(P, TILES),
        "dst": np.concatenate([np.full(1, -1, np.asarray(dst).dtype), rows(dst, ROWS, NODES - 1)]),
        "edge_w": rows(np.asarray(edge_weight1).reshape(-1), ROWS).reshape(P, TILES),
        "ea64": rows(edge_attr_64, ROWS),
        "ea16": rows(edge_attr_16, ROWS),
        "w1t": np.concatenate([np.asarray(L1_gnn_W).T, np.asarray(L1_gnn_b).reshape(1, D)]),
        "wlr": np.concatenate([np.concatenate([np.asarray(L2_gnn_Wl), np.asarray(L2_gnn_Wr)], axis=2),
                               np.concatenate([np.asarray(L2_gnn_bl), np.asarray(L2_gnn_br)], axis=1)
                               .reshape(LAYERS, 1, 2 * D)], axis=1),
        "att": np.asarray(L2_gnn_att).reshape(1, -1),
        "bias2": np.asarray(L2_gnn_bias).reshape(1, -1),
        "w3": np.asarray(L3_gnn_W),
        "wa": np.asarray(L3_gnn_w_att).reshape(1, -1),
        "bias3": np.asarray(L3_gnn_bias).reshape(1, D),
    }
    return {k: np.ascontiguousarray(a) for k, a in out.items()}


def kernel(**inputs):
    import numpy as np
    import concourse.bacc as bacc
    from concourse.bass_utils import run_bass_kernel_spmd

    nc = bacc.Bacc("TRN2", target_bir_lowering=False, num_devices=1)
    arrays, io = {}, {}
    for name, a in laid_out(**inputs).items():
        arrays[f"in_{name}"] = a
        io[name] = nc.dram_tensor(f"in_{name}", a.shape, mybir.dt.from_np(a.dtype), kind="ExternalInput").ap()
    io["out"] = nc.dram_tensor("out_nodes", (P, KN * D), F32, kind="ExternalOutput").ap()
    build_program(nc, io)
    result = run_bass_kernel_spmd(nc, [arrays], core_ids=[0])
    return np.ascontiguousarray(result.results[0]["out_nodes"].reshape(NODES, D)[:N])
```
